# Optimizing a Trainium2 kernel written in Bass

```python
import numpy as np
import jax
import jax.numpy as jnp

def _softmax(x, axis=-1):
    return jax.nn.softmax(x, axis=axis)
def _gelu(x):
    return jax.nn.gelu(x, approximate=True)
def _silu(x):
    return jax.nn.silu(x)
def _sigmoid(x):
    return jax.nn.sigmoid(x)
def _layernorm(x, axis=-1, eps=1e-5):
    m = jnp.mean(x, axis=axis, keepdims=True)
    v = jnp.var(x, axis=axis, keepdims=True)
    return (x - m) / jnp.sqrt(v + eps)
def _scatter_add(tgt, idx, src, axis=0):
    return tgt.at[idx].add(src)
def _segment_sum(src, seg, n):
    return jax.ops.segment_sum(src, seg, n)

kernel_name = 'mk_conv_seq_d1_conv_nhwc512_ba675f'

def setup_inputs(seed: int = 0):
    np.random.seed(seed)
    _w = jnp.asarray
    def _rec_inputs():
        import jax
        import jax.numpy as jnp
        _gk = jax.random.key(seed)
        x = 7.22e-05 + 1 * jax.random.normal(jax.random.fold_in(_gk, 1), (16, 32, 32, 512), jnp.float32)
        return x
    x = _rec_inputs()
    def _L0_conv_setup():
        import jax, jax.numpy as jnp
        import numpy as np
        GROUPS = 32
        EPS = 1e-05
        HEAD_DIM = 64

        def group_norm(x, gamma, beta):
            B, L, C = x.shape
            g = x.reshape(B, L, GROUPS, C // GROUPS)
            mean = g.mean(axis=(1, 3), keepdims=True)
            var = g.var(axis=(1, 3), keepdims=True)
            g = (g - mean) * jax.lax.rsqrt(var + EPS)
            return g.reshape(B, L, C) * gamma + beta
        key = jax.random.key(seed)
        ks = jax.random.split(key, 4)
        B, H, W, C = (16, 32, 32, 512)
        x = jax.random.normal(ks[0], (B, H, W, C), dtype=jnp.float32)
        timesteps = jax.random.randint(ks[1], (B,), 0, 1000)
        gamma = jnp.ones((C,), jnp.float32)
        beta = jnp.zeros((C,), jnp.float32)
        w_qkv = jax.random.normal(ks[2], (C, 3 * C), dtype=jnp.float32) * (1.0 / np.sqrt(C))
        b_qkv = jnp.zeros((3 * C,), jnp.float32)
        w_out = jax.random.normal(ks[3], (C, C), dtype=jnp.float32) * (1.0 / np.sqrt(C))
        b_out = jnp.zeros((C,), jnp.float32)
        return {'x': x, 'timesteps': timesteps, 'gamma': gamma, 'beta': beta, 'w_qkv': w_qkv, 'b_qkv': b_qkv, 'w_out': w_out, 'b_out': b_out}
    _L0_conv_all = _L0_conv_setup()
    _L0_conv_in = {k: v for k, v in _L0_conv_all.items() if k in ('timesteps', 'gamma', 'beta', 'w_qkv', 'b_qkv', 'w_out', 'b_out', )}
    del _L0_conv_all

    return {
        "x": x,
        "L0_conv_timesteps": _L0_conv_in["timesteps"],
        "L0_conv_gamma": _L0_conv_in["gamma"],
        "L0_conv_beta": _L0_conv_in["beta"],
        "L0_conv_w_qkv": _L0_conv_in["w_qkv"],
        "L0_conv_b_qkv": _L0_conv_in["b_qkv"],
        "L0_conv_w_out": _L0_conv_in["w_out"],
        "L0_conv_b_out": _L0_conv_in["b_out"],
    }

def reference(x, L0_conv_timesteps, L0_conv_gamma, L0_conv_beta, L0_conv_w_qkv, L0_conv_b_qkv, L0_conv_w_out, L0_conv_b_out):
    import jax
    import jax.numpy as jnp
    def _L0_conv_ref(x, timesteps, gamma, beta, w_qkv, b_qkv, w_out, b_out):
        import jax, jax.numpy as jnp
        import numpy as np
        GROUPS = 32
        EPS = 1e-05
        HEAD_DIM = 64

        def group_norm(x, gamma, beta):
            B, L, C = x.shape
            g = x.reshape(B, L, GROUPS, C // GROUPS)
            mean = g.mean(axis=(1, 3), keepdims=True)
            var = g.var(axis=(1, 3), keepdims=True)
            g = (g - mean) * jax.lax.rsqrt(var + EPS)
            return g.reshape(B, L, C) * gamma + beta
        B, H, W, C = x.shape
        L = H * W
        nh = C // HEAD_DIM
        factor = jnp.asarray(1.0 / np.sqrt(np.sqrt(HEAD_DIM)), x.dtype)
        xf = x.reshape(B, L, C)
        qkv = group_norm(xf, gamma, beta) @ w_qkv + b_qkv
        q, k, v = jnp.split(qkv, 3, axis=-1)

        def heads(t):
            return t.reshape(B, L, nh, HEAD_DIM).transpose(0, 2, 1, 3)
        q, k, v = (heads(q) * factor, heads(k) * factor, heads(v))
        scores = jnp.einsum('bhqd,bhkd->bhqk', q, k)
        attn = jax.nn.softmax(scores, axis=-1)
        out = jnp.einsum('bhqk,bhkd->bhqd', attn, v)
        out = out.transpose(0, 2, 1, 3).reshape(B, L, C)
        h = out @ w_out + b_out
        return (xf + h).reshape(B, H, W, C)

    def _gn(v, G=32, eps=1e-5):
        B_, H_, W_, C_ = v.shape
        g = v.reshape(B_, H_, W_, G, C_ // G)
        m = jnp.mean(g, axis=(1, 2, 4), keepdims=True)
        s = jnp.var(g, axis=(1, 2, 4), keepdims=True)
        return ((g - m) / jnp.sqrt(s + eps)).reshape(v.shape)

    def _ln_c(v, eps=1e-6):
        m = jnp.mean(v, axis=-1, keepdims=True)
        s = jnp.var(v, axis=-1, keepdims=True)
        return (v - m) / jnp.sqrt(s + eps)

    def _ln_t(v, eps=1e-5):
        m = jnp.mean(v, axis=-1, keepdims=True)
        s = jnp.var(v, axis=-1, keepdims=True)
        return (v - m) / jnp.sqrt(s + eps)

    def _to_tokens(v):
        B_, H_, W_, C_ = v.shape
        return v.reshape(B_, H_ * W_, C_)
    def _from_tokens(t, like):
        return t.reshape(like.shape)

    x = _L0_conv_ref(x, L0_conv_timesteps, L0_conv_gamma, L0_conv_beta, L0_conv_w_qkv, L0_conv_b_qkv, L0_conv_w_out, L0_conv_b_out)
    return x


_drawn_inputs = setup_inputs


def setup_inputs(seed=0):
    import zlib

    import numpy as np

    out = dict(_drawn_inputs(seed))
    spreads = {'L0_conv_gamma': (1.0, 0.2),
     'L0_conv_beta': (0.0, 0.1),
     'L0_conv_b_qkv': (0.0, 0.1),
     'L0_conv_b_out': (0.0, 0.1)}
    factors = {}
    for name, (base, spread) in spreads.items():
        noise = np.random.default_rng([zlib.crc32(name.encode()), seed]).standard_normal(out[name].shape)
        drawn = base * np.exp(spread * noise) if base else spread * noise
        out[name] = jnp.asarray(drawn.astype(out[name].dtype))
    for name, factor in factors.items():
        out[name] = (out[name] * factor).astype(out[name].dtype)
    return out
```

```python
from contextlib import ExitStack

import concourse.bass as bass
from concourse import mybir

F32 = mybir.dt.float32
F32R = mybir.dt.float32r
ALU = mybir.AluOpType
ACT = mybir.ActivationFunctionType
AX_X = mybir.AxisListType.X

P = 128
BATCH, HH, WW, C = 16, 32, 32, 512
L = HH * WW
D = 64
NH = C // D
NPAIR = NH // 2
CT = C // P
TT = L // P
HALF = 512
NHALF = L // HALF
GROUPS = 32
GC = C // GROUPS
EPS = 1e-5
SCALE = 1.0 / 8.0
STEPS = NH * TT
LAG = 2
NSLOT = 4
NRES = 4
QK_ITEMS = 2 * NHALF


def schedule(prepare_next):
    ahead = [[] for _ in range(STEPS + 1)]
    behind = [[] for _ in range(STEPS + 1)]

    def project(pair, steps):
        for i in range(QK_ITEMS):
            job = (pair, i // NHALF, i % NHALF)
            a, b = steps[2 * i:2 * i + 2]
            ahead[a] += [("qk_part", *job, 0), ("qk_part", *job, 1)]
            ahead[b] += [("qk_part", *job, 2), ("qk", *job)]

    def maxima(h, steps):
        for qt, s in enumerate(steps):
            ahead[s].insert(0, ("max", h, qt, 0))
            (behind if s < STEPS else ahead)[s].append(("max", h, qt, 1))

    for pair in range(1, NPAIR):
        end = 16 * pair - 10
        project(pair, [max(0, s) for s in (end - 8, end - 7, end - 5, end - 4, end - 3, end - 2, end - 1, end)])
    for h in range(1, NH):
        at = 8 * (h - 1) - 1
        maxima(h, [max(0, at), max(0, at + 1), at + 2, at + 3, at + 4, at + 5, at + 6, at + 6])
        ahead[at + 7].append(("max_row", h))
    for h in range(NH - 1):
        ahead[8 * h + 10].append(("denominator", h))
        ahead[8 * h + 11].append(("reciprocal_row", h))
    tail = ahead[STEPS]
    if prepare_next:
        for tt in range(TT):
            ahead[39 + tt].append(("x", tt))
        ahead[47].append(("group_mean",))
        ahead[48].append(("group_var",))
        project(0, range(50, 58))
        maxima(0, [58, 59, 60, 61, 62, 63, 63, 63])
        tail += [("v", 0), ("v", 1), ("max_row", 0), ("v", 2), ("denominator", NH - 1), ("v", 3)]
        tail += [("reciprocal_row", NH - 1)] + [("v", tt) for tt in range(4, TT)]
    else:
        tail += [("denominator", NH - 1), ("reciprocal_row", NH - 1)]
    tail += [("out", tt) for tt in range(TT)]
    return ahead, behind


def first_schedule():
    jobs = [("x", tt) for tt in range(TT)] + [("group_mean",), ("group_var",)]
    for i in range(QK_ITEMS):
        job = (0, i // NHALF, i % NHALF)
        jobs += [("qk_part", *job, ct) for ct in range(CT - 1)] + [("qk", *job)]
    jobs += [("max", 0, qt, half) for qt in range(TT) for half in range(NHALF)]
    return [jobs + [("max_row", 0)] + [("v", tt) for tt in range(TT)]], [[]]


class Jobs:

    def __init__(self, schedule, alternate):
        self.ahead, self.behind = schedule
        self.bank, self.no, self.total = {}, {}, [0, 0]
        for a, b in zip(self.ahead, self.behind):
            for job in (j for j in a + b if j[0] != "qk_part"):
                if alternate:
                    bank = len(self.no) % 2
                elif job[0] in ("v", "out"):
                    bank = job[1] % 2
                else:
                    bank = 0 if job[0] == "qk" else 1
                self.bank[job], self.no[job] = bank, self.total[bank]
                self.total[bank] += 1


FIRST = Jobs(first_schedule(), True)
LOOP = Jobs(schedule(True), False)
LAST = Jobs(schedule(False), False)


class Body:

    def __init__(self, b, prepares, jobs, loops):
        self.b = b
        self.prepares = prepares
        self.jobs, self.loops = jobs, loops

    def bank(self, job):
        return self.jobs.bank[("qk", *job[1:4]) if job[0] == "qk_part" else job]

    def before(self, bank):
        return 0 if self.loops is None else self.loops * LOOP.total[bank] + FIRST.total[bank]

    def free(self, job):
        return self.before(self.bank(job)) + self.jobs.no[job]

    def done(self, job):
        return self.before(self.bank(job)) + (self.jobs.no[job] + 1)


def build(nc, x, gamma, beta, w_qkv, b_qkv, w_out, b_out, out):
    x_flat = x.rearrange("b h w c -> (b h w c)")
    out_flat = out.rearrange("b h w c -> (b h w c)")

    with ExitStack() as ctx:
        def sb(name, shape, dt=F32):
            return ctx.enter_context(nc.sbuf_tensor(name, shape, dt))

        def ps(name, shape):
            return ctx.enter_context(nc.psum_tensor(name, shape, F32))

        def sem(name):
            return ctx.enter_context(nc.semaphore(name))

        wqkv = sb("wqkv", [P, CT, 3 * C])
        wout = sb("wout", [P, CT, C])
        ident = sb("ident", [P, P])
        group = sb("group", [P, P])
        ones = sb("ones", [P, 2])
        bias_all = sb("bias_all", [P, C])
        bv = sb("bv", [P, CT])
        gamma_c = sb("gamma_c", [P, CT])
        beta_c = sb("beta_c", [P, CT])
        bqk = sb("bqk", [P, 2, NPAIR])
        bqk_odd = sb("bqk_odd", [D, 2, NPAIR])
        xt = sb("xt", [P, 2, C])
        xn = sb("xn", [P, CT, L])
        bn = sb("bn", [P, CT, NHALF, 6])
        carrier = sb("carrier", [P, 1])
        chan = sb("chan", [P, CT, 2])
        grp = sb("grp", [P, CT, 2])
        dev = sb("dev", [P, CT])
        dev2 = sb("dev2", [P, CT])
        gvar = sb("gvar", [P, CT])
        power = sb("power", [P, CT])
        rstd = sb("rstd", [P, CT])
        mul = sb("mul", [P, CT])
        off = sb("off", [P, CT])
        moff = sb("moff", [P, CT])
        k_stack = sb("k_stack", [P, NSLOT, L], F32R)
        k_aug = sb("k_aug", [D + 1, NSLOT, L], F32R)
        q_twin = sb("q_twin", [P, NSLOT, L], F32R)
        q_aug = sb("q_aug", [D + 1, NSLOT, L], F32R)
        v_stack = sb("v_stack", [P, TT, NPAIR, 4, D], F32R)
        mx = sb("mx", [P, TT, NHALF])
        mrow = sb("mrow", [P, TT])
        neg_max = sb("neg_max", [TT, P], F32R)
        prob = sb("prob", [P, 2, L])
        prob_hi = sb("prob_hi", [P, 2, L], F32R)
        prob_lo = sb("prob_lo", [P, 2, L], F32R)
        key_sum = sb("key_sum", [P, 2, L])
        recip = sb("recip", [P, TT])
        recip_t = sb("recip_t", [TT, P])
        side = sb("side", [P, L])
        o_cat = sb("o_cat", [P, NPAIR, L])

        recip_dram = nc.dram_tensor("recip_dram", [TT, P], F32, kind="Internal").ap()

        def res(tt):
            return prob[:, (tt % NRES) // 2, (tt % 2) * HALF:(tt % 2 + 1) * HALF]

        scores = ps("scores", [P, 2, L])
        pv = ps("pv", [P, L])
        spare = ps("spare", [P, 2, HALF])

        s_build = sem("s_build")
        s_load = sem("s_load")
        s_const = sem("s_const")
        s_x_load = [sem(f"s_x_load{i}") for i in range(2)]
        s_stat = sem("s_stat")
        s_rstd = sem("s_rstd")
        s_xn = sem("s_xn")
        s_filled = [sem(f"s_filled{i}") for i in range(2)]
        s_taken = [sem(f"s_taken{i}") for i in range(2)]
        s_qk_hi = sem("s_qk_hi")
        s_v_hi = sem("s_v_hi")
        s_bias = sem("s_bias")
        s_bias_ps = sem("s_bias_ps")
        s_rowmax = sem("s_rowmax")
        s_shift = sem("s_shift")
        s_scores = sem("s_scores")
        s_exp = sem("s_exp")
        s_hi = sem("s_hi")
        s_lo = sem("s_lo")
        s_sum = sem("s_sum")
        s_pv = sem("s_pv")
        s_o_low = sem("s_o_low")
        s_o = sem("s_o")
        s_recip_row = sem("s_recip_row")
        s_recip_all = sem("s_recip_all")
        s_o_norm = sem("s_o_norm")
        s_res = [sem(f"s_res{i}") for i in range(NRES)]
        s_res_bias = sem("s_res_bias")
        s_store = [sem(f"s_store{i}") for i in range(NRES)]

        NLOAD = 16 * (2 * CT + 2 + 2 * 2 + 2)
        NCONST = 4
        NSTAT = 7
        NSUM = TT - 1

        first = Body(None, 0, FIRST, None)
        last = Body(BATCH - 1, None, LAST, BATCH - 1)

        def looped(b):
            return Body(b, b + 1, LOOP, b)

        def half(i):
            return slice(i * HALF, (i + 1) * HALF)

        def tile(i):
            return slice(i * P, (i + 1) * P)

        def tokens(dram, start):
            return dram[bass.ds(start, P * C)].rearrange("(p c) -> p c", c=C)

        def image_of(body, h):
            return body.prepares if h == 0 else body.b

        block = ctx.enter_context(nc.Block())

        @block.sync
        def _(sp):
            def early(value):
                return value if isinstance(value, int) else sp.snap(value)

            def start_of(n, tt):
                return early(n * (L * C) + tt * P * C)

            def load_x(body, tt):
                n = body.prepares
                start = start_of(n, tt)
                if tt >= 2:
                    job = ("x", tt - 2)
                    sp.wait_ge(s_taken[body.bank(job)], body.done(job))
                elif body is not first:
                    sp.wait_ge(s_v_hi, n * TT)
                sp.dma_start(xt[:, tt % 2, :], tokens(x_flat, start)).then_inc(s_x_load[tt % 2], 16)

            def shift_row(body, job):
                h = job[1]
                sp.wait_ge(s_taken[body.bank(job)], body.done(job))
                sp.dma_start(q_aug[D:D + 1, h % NSLOT, :].bitcast(F32).rearrange("a (t p) -> a t p", p=P),
                             neg_max[:, :].bitcast(F32)
                             ).then_inc(s_shift, 16)

            def recip_rows(body, job):
                h = job[1]
                rows = slice(D * (h % 2), D * (h % 2) + D)
                sp.wait_ge(s_taken[body.bank(job)], body.done(job))
                sp.dma_start(recip_dram[:, :], recip_t[:, :]).then_inc(s_recip_row, 16)
                sp.wait_ge(s_recip_row, body.b * (16 * NH) + 16 * (h + 1))
                sp.dma_start(side[rows, :],
                             recip_dram.rearrange("(a t) p -> a (t p)", a=1).broadcast_to([D, L])
                             ).then_inc(s_recip_all, 16)

            def load_res(body, tt):
                b = body.b
                start = start_of(b, tt)
                if tt < NRES:
                    steps = early(b * STEPS + STEPS)
                    sums = early(b * (NH * NSUM) + NH * NSUM)
                    sp.wait_ge(s_hi, steps)
                    sp.wait_ge(s_lo, steps)
                    sp.wait_ge(s_sum, sums)
                else:
                    sp.wait_ge(s_store[tt % NRES], b * 32 + 16)
                sp.dma_start(res(tt), tokens(x_flat, start)).then_inc(s_res[tt % NRES], 16)

            def store(body, job):
                tt = job[1]
                start = start_of(body.b, tt)
                sp.wait_ge(s_taken[body.bank(job)], body.done(job))
                sp.dma_start(tokens(out_flat, start), res(tt)).then_inc(s_store[tt % NRES], 16)

            def run(body):
                if body is not last:
                    load_x(body, 0)
                    load_x(body, 1)
                for s, (ahead, behind) in enumerate(zip(body.jobs.ahead, body.jobs.behind)):
                    if s == STEPS:
                        for tt in range(NRES):
                            load_res(body, tt)
                    for job in ahead + behind:
                        if job[0] == "x" and job[1] + 2 < TT:
                            load_x(body, job[1] + 2)
                        if job[0] == "max_row":
                            shift_row(body, job)
                        if job[0] == "reciprocal_row":
                            recip_rows(body, job)
                        if job[0] == "out":
                            store(body, job)
                            if job[1] + NRES < TT:
                                load_res(body, job[1] + NRES)

            for ct in range(CT):
                sp.dma_start(wqkv[:, ct, :], w_qkv[tile(ct), :]).then_inc(s_load, 16)
                sp.dma_start(wout[:, ct, :], w_out[tile(ct), :]).then_inc(s_load, 16)
            with nc.allow_non_contiguous_dma("a few small vectors, once"):
                sp.dma_start(gamma_c[:, :], gamma.rearrange("(t p) -> p t", p=P)).then_inc(s_load, 16)
                sp.dma_start(beta_c[:, :], beta.rearrange("(t p) -> p t", p=P)).then_inc(s_load, 16)
                sp.dma_start(bv[:, :], b_qkv[2 * C:3 * C].rearrange("(t p) -> p t", p=P)).then_inc(s_load, 16)
                for j in range(2):
                    part = b_qkv[j * C:(j + 1) * C].rearrange("(t p) -> p t", p=P)
                    sp.dma_start(bqk[:, j, :], part).then_inc(s_load, 16)
                    sp.dma_start(bqk_odd[:, j, :], part[D:P, :]).then_inc(s_load, 16)
            sp.dma_start(bias_all[:, :], b_out.rearrange("(a c) -> a c", a=1).broadcast_to([P, C])
                         ).then_inc(s_load, 16)
            run(first)
            with sp.Fori(0, BATCH - 1) as b:
                run(looped(b))
            run(last)
            for i in range(NRES):
                sp.wait_ge(s_store[i], BATCH * 32)

        @block.tensor
        def _(pe):
            def project(job, bank, ct):
                pair, which, i = job[1:4]
                return pe.matmul(bank, wqkv[:, ct, which * C + pair * P:which * C + (pair + 1) * P],
                                 xn[:, ct, half(i)], start=(ct == 0), stop=(ct == CT - 1), skip_group_check=True)

            def do(body, job):
                kind = job[0]
                if kind == "qk_part":
                    whole = ("qk", *job[1:4])
                    bank = spare[:, body.bank(whole), :]
                    if job[4] == 0:
                        if not (body is first and body.jobs.no[whole] == 0):
                            pe.wait_ge(s_taken[body.bank(whole)], body.free(whole))
                        if job[1] == 0:
                            pe.wait_ge(s_xn, body.prepares * CT + CT)
                    project(whole, bank, job[4])
                    return
                if kind == "qk":
                    project(job, spare[:, body.bank(job), :], CT - 1).then_inc(s_filled[body.bank(job)], 1)
                    return
                bank = spare[:, body.bank(job), :]
                if not (body is first and body.jobs.no[job] == 0):
                    pe.wait_ge(s_taken[body.bank(job)], body.free(job))
                if kind == "x":
                    tt = job[1]
                    pe.wait_ge(s_x_load[tt % 2], body.prepares * (8 * TT) + 16 * (tt // 2 + 1))
                    for ct in range(CT):
                        mm = pe.transpose(bank[:, tile(ct)], xt[:, tt % 2, tile(ct)], ident[:, :])
                elif kind == "group_mean":
                    pe.wait_ge(s_stat, body.prepares * NSTAT + 2)
                    mm = pe.matmul(bank[:, 0:2 * CT], group[:, :], chan[:, :, :].rearrange("p t s -> p (t s)"),
                                   start=True, stop=True)
                elif kind == "group_var":
                    pe.wait_ge(s_stat, body.prepares * NSTAT + 4)
                    mm = pe.matmul(bank[:, 0:CT], group[:, :], dev2[:, :], start=True, stop=True)
                elif kind == "v":
                    for ct in range(CT):
                        mm = pe.matmul(bank, xn[:, ct, tile(job[1])], wqkv[:, ct, 2 * C:3 * C],
                                       start=(ct == 0), stop=(ct == CT - 1))
                elif kind == "max":
                    _, h, qt, i = job
                    if h % 2 == 0 and qt == 0 and i == 0:
                        made = [("qk", h // 2, which, j) for which in range(2) for j in range(NHALF)]
                        other = [j for j in made if body.bank(j) != body.bank(job)]
                        if other:
                            pe.wait_ge(s_taken[body.bank(other[-1])], body.done(other[-1]))
                    mm = pe.matmul(bank, q_twin[:, h % NSLOT, tile(qt)], k_stack[:, h % NSLOT, half(i)],
                                   start=True, stop=True)
                elif kind == "max_row":
                    h = job[1]
                    pe.wait_ge(s_rowmax, image_of(body, h) * NH + (h + 1))
                    mm = pe.transpose(bank[0:TT, 0:P], mrow[:, :], ident[:, :])
                elif kind == "denominator":
                    h = job[1]
                    pe.wait_ge(s_sum, body.b * (NH * NSUM) + NSUM * (h + 1))
                    for qt in range(TT):
                        mm = pe.matmul(bank[:, qt:qt + 1], key_sum[:, h % 2, tile(qt)], ones[:, 0:1],
                                       start=True, stop=True)
                elif kind == "reciprocal_row":
                    pe.wait_ge(s_o, body.b * NH + (job[1] + 1))
                    made = ("denominator", job[1])
                    if body.bank(made) != body.bank(job):
                        pe.wait_ge(s_taken[body.bank(made)], body.done(made))
                    mm = pe.transpose(bank[0:TT, 0:P], recip[:, :], ident[:, :])
                elif kind == "out":
                    if job[1] == 0:
                        pe.wait_ge(s_o_norm, body.b * NH + NH)
                    for ct in range(CT):
                        mm = pe.matmul(bank, o_cat[:, ct, tile(job[1])], wout[:, ct, :],
                                       start=(ct == 0), stop=(ct == CT - 1))
                mm.then_inc(s_filled[body.bank(job)], 1)

            def step_scores(b, s):
                h, kt = s // TT, s % TT
                slot = h % NSLOT
                if kt == 0:
                    pe.wait_ge(s_shift, b * (16 * NH) + 16 * (h + 1))
                pe.wait_ge(s_exp, b * STEPS + max(s - 1, 0))
                for i in range(NHALF):
                    pe.matmul(scores[:, s % 2, half(i)], k_stack[:, slot, tile(kt)], q_twin[:, slot, half(i)],
                              start=True, stop=False)
                for i in range(NHALF):
                    mm = pe.matmul(scores[:, s % 2, half(i)], k_aug[:, slot, tile(kt)], q_aug[:, slot, half(i)],
                                   start=False, stop=True)
                mm.then_inc(s_scores, 1)

            def step_pv(b, s):
                h, kt = s // TT, s % TT
                if kt == 0:
                    pe.wait_ge(s_o, b * NH + h)
                v = v_stack[:, kt, h // 2, 2 * (h % 2):2 * (h % 2) + 2, :].rearrange("p a d -> p (a d)")
                pe.wait_ge(s_hi, b * STEPS + (s + 1))
                for i in range(NHALF):
                    pe.matmul(pv[:, half(i)], v, prob_hi[:, s % 2, half(i)], start=(kt == 0), stop=False)
                pe.wait_ge(s_lo, b * STEPS + (s + 1))
                for i in range(NHALF):
                    mm = pe.matmul(pv[:, half(i)], v, prob_lo[:, s % 2, half(i)], start=False,
                                   stop=(kt == TT - 1))
                mm.then_inc(s_pv, 1)

            def run(body):
                for bank in range(2):
                    pe.wait_ge(s_taken[bank], body.before(bank))
                for s, (ahead, behind) in enumerate(zip(body.jobs.ahead, body.jobs.behind)):
                    if s < STEPS:
                        step_scores(body.b, s)
                    for n, job in enumerate(ahead):
                        if s == STEPS and n < LAG:
                            step_pv(body.b, s - LAG + n)
                        do(body, job)
                    if LAG <= s < STEPS:
                        step_pv(body.b, s - LAG)
                    for job in behind:
                        do(body, job)

            pe.wait_ge(s_load, NLOAD)
            pe.wait_ge(s_const, NCONST)
            pe.wait_ge(s_bias, 5)
            for ct in range(CT):
                mm = pe.matmul(pv[:, half(0)], side[:, tile(ct)], wout[:, ct, :],
                               start=(ct == 0), stop=(ct == CT - 1))
            mm.then_inc(s_bias_ps, 1)
            for job in FIRST.ahead[0]:
                do(first, job)
            with pe.Fori(0, BATCH - 1) as b:
                run(looped(b))
            run(last)

        @block.scalar
        def _(act):
            def do(body, job):
                kind = job[0]
                bank = spare[:, body.bank(job), :]
                taken = s_taken[body.bank(job)]
                if kind in ("x", "qk", "v", "max_row", "reciprocal_row"):
                    act.wait_ge(s_filled[body.bank(job)], body.done(job))
                if kind == "x":
                    act.activation(xn[:, :, tile(job[1])], bank.rearrange("p (t c) -> p t c", t=CT), ACT.Copy
                                   ).then_inc(taken, 1)
                if kind == "qk":
                    _, pair, which, i = job
                    for e in range(2):
                        slot = (2 * pair + e) % NSLOT
                        rows = slice(D * e, D * e + D)
                        for to in ((q_twin[0:D, slot, half(i)], q_twin[D:P, slot, half(i)]),
                                   (k_stack[0:D, slot, half(i)], k_aug[0:D, slot, half(i)]))[which]:
                            hi = act.activation(to, bank[rows, :], ACT.Identity, bias=bqk[rows, which, pair:pair + 1])
                    hi.then_inc(s_qk_hi, 1)
                if kind == "v":
                    act.activation(v_stack[:, job[1], :, 0::3, :],
                                   bank.rearrange("p (a e d) -> p a e d", e=2, d=D), ACT.Copy).then_inc(s_v_hi, 1)
                if kind == "max_row":
                    h = job[1]
                    if body is not first:
                        act.wait_ge(s_shift, image_of(body, h) * (16 * NH) + 16 * h)
                    act.activation(neg_max[:, :], bank[0:TT, 0:P], ACT.Copy, scale=-1.0).then_inc(taken, 1)
                if kind == "reciprocal_row":
                    act.wait_ge(s_recip_row, body.b * (16 * NH) + 16 * job[1])
                    act.activation(recip_t[:, :], bank[0:TT, 0:P], ACT.Copy).then_inc(taken, 1)

            def step_exp(b, s):
                act.wait_ge(s_scores, b * STEPS + (s + 1))
                if s < 2:
                    for i in range(NRES):
                        act.wait_ge(s_store[i], b * 32)
                else:
                    h, kt = (s - 2) // TT, (s - 2) % TT
                    act.wait_ge(s_lo, b * STEPS + (s - 1))
                    act.wait_ge(s_sum, b * (NH * NSUM) + NSUM * h + max(kt, 1))
                act.activation(prob[:, s % 2, :], scores[:, s % 2, :], ACT.Exp, scale=SCALE).then_inc(s_exp, 1)

            def step_hi(b, s):
                act.wait_ge(s_exp, b * STEPS + (s + 1))
                act.wait_ge(s_pv, b * STEPS + max(s - 1, 0))
                act.activation(prob_hi[:, s % 2, :], prob[:, s % 2, :], ACT.Copy).then_inc(s_hi, 1)

            def take_o_low(b, h):
                act.wait_ge(s_pv, b * STEPS + TT * (h + 1))
                act.wait_ge(s_o_norm, b * NH + max(h - 1, 0))
                to, frm = D * (h % 2), D * (1 - h % 2)
                act.activation(side[to:to + D, :], pv[frm:frm + D, :], ACT.Copy).then_inc(s_o_low, 1)

            def run(body):
                for s, (ahead, behind) in enumerate(zip(body.jobs.ahead, body.jobs.behind)):
                    if s < STEPS:
                        step_exp(body.b, s)
                    else:
                        take_o_low(body.b, NH - 1)
                    for job in ahead:
                        do(body, job)
                    if s < STEPS:
                        if s > TT and (s - LAG + 1) % TT == 0:
                            take_o_low(body.b, (s - LAG + 1) // TT - 1)
                        step_hi(body.b, s)
                    for job in behind:
                        do(body, job)

            act.wait_ge(s_load, NLOAD)
            for job in FIRST.ahead[0]:
                do(first, job)
            with act.Fori(0, BATCH - 1) as b:
                run(looped(b))
            run(last)

        @block.vector
        def _(dve):
            def do(body, job):
                kind, n = job[0], body.prepares
                bank = spare[:, body.bank(job), :]
                taken = s_taken[body.bank(job)]
                if kind in ("group_mean", "group_var", "max", "denominator", "out"):
                    dve.wait_ge(s_filled[body.bank(job)], body.done(job))
                if kind == "x" and job[1] == TT - 1:
                    for tt in (TT - 2, TT - 1):
                        dve.wait_ge(s_taken[body.bank(("x", tt))], body.done(("x", tt)))
                    for ct in range(CT):
                        for i in range(NHALF):
                            a = dve.bn_stats(bn[:, ct, i, :], xn[:, ct, half(i)])
                    a.then_inc(s_stat, 1)
                    dve.wait_ge(s_stat, n * NSTAT + 1)
                    dve.memset(carrier[:, :], 0.0)
                    for ct in range(CT):
                        a = dve.bn_aggr(chan[:, ct, :], bn[:, ct, :, :])
                    a.then_inc(s_stat, 1)
                if kind == "group_mean":
                    dve.tensor_copy(grp[:, :, :].rearrange("p t s -> p (t s)"), bank[:, 0:2 * CT]).then_inc(taken, 1)
                    dve.wait_ge(taken, body.done(job))
                    dve.tensor_tensor(dev[:, :], chan[:, :, 0], grp[:, :, 0], ALU.subtract).then_inc(s_stat, 1)
                    dve.wait_ge(s_stat, n * NSTAT + 3)
                    dve.tensor_tensor(dev2[:, :], dev[:, :], dev[:, :], ALU.mult).then_inc(s_stat, 1)
                if kind == "group_var":
                    dve.scalar_tensor_tensor(out=gvar[:, :], in0=bank[:, 0:CT], scalar=EPS, in1=grp[:, :, 1],
                                             op0=ALU.add, op1=ALU.add).then_inc(taken, 1)
                    dve.wait_ge(s_rstd, n + 1)
                    dve.tensor_tensor(mul[:, :], rstd[:, :], gamma_c[:, :], ALU.mult).then_inc(s_stat, 1)
                    dve.wait_ge(s_stat, n * NSTAT + 5)
                    dve.tensor_tensor(moff[:, :], grp[:, :, 0], mul[:, :], ALU.mult).then_inc(s_stat, 1)
                    dve.wait_ge(s_stat, n * NSTAT + 6)
                    dve.tensor_tensor(off[:, :], beta_c[:, :], moff[:, :], ALU.subtract).then_inc(s_stat, 1)
                    dve.wait_ge(s_stat, n * NSTAT + 7)
                    for ct in range(CT):
                        dve.tensor_scalar(xn[:, ct, :], xn[:, ct, :], mul[:, ct:ct + 1], off[:, ct:ct + 1],
                                          ALU.mult, ALU.add).then_inc(s_xn, 1)
                if kind == "qk":
                    _, pair, which, i = job
                    before = image_of(body, pair) * (NPAIR * QK_ITEMS)
                    dve.wait_ge(s_qk_hi, before + (QK_ITEMS * pair + which * NHALF + i + 1))
                    for e in range(2):
                        slot = (2 * pair + e) % NSLOT
                        hi = (q_twin, k_stack)[which][0:D, slot, half(i)]
                        lo = (q_aug[0:D, slot, half(i)], k_stack[D:P, slot, half(i)])[which]
                        a = dve.scalar_tensor_tensor(out=lo, in0=bank[D * e:D * e + D, :],
                                                     scalar=(bqk, bqk_odd)[e][0:D, which, pair:pair + 1], in1=hi,
                                                     op0=ALU.add, op1=ALU.subtract)
                    a.then_inc(taken, 1)
                if kind == "v":
                    tt = job[1]
                    dve.wait_ge(s_v_hi, n * TT + (tt + 1))
                    dve.tensor_tensor(v_stack[:, tt, :, 1:3, :], bank.rearrange("p (a e d) -> p a e d", e=2, d=D),
                                      v_stack[:, tt, :, 0::3, :], ALU.subtract).then_inc(taken, 1)
                if kind == "max":
                    _, h, qt, i = job
                    dve.tensor_reduce(mx[:, qt, i:i + 1], bank, AX_X, ALU.max).then_inc(taken, 1)
                    if qt == TT - 1 and i == NHALF - 1:
                        for j in range(NHALF):
                            end = ("max", h, qt, j)
                            dve.wait_ge(s_taken[body.bank(end)], body.done(end))
                        dve.tensor_tensor(mrow[:, :], mx[:, :, 0], mx[:, :, 1], ALU.max).then_inc(s_rowmax, 1)
                if kind == "denominator":
                    dve.reciprocal(recip[:, :], bank[:, 0:TT]).then_inc(taken, 1)
                if kind == "out":
                    tt = job[1]
                    dve.wait_ge(s_res_bias, body.b * TT + (tt + 1))
                    dve.tensor_tensor(res(tt), bank, res(tt), ALU.add).then_inc(taken, 1)

            def step_lo(b, s):
                dve.wait_ge(s_hi, b * STEPS + (s + 1))
                dve.wait_ge(s_pv, b * STEPS + max(s - 1, 0))
                dve.tensor_tensor(prob_lo[:, s % 2, :], prob[:, s % 2, :], prob_hi[:, s % 2, :], ALU.subtract
                                  ).then_inc(s_lo, 1)

            def add_o(b, h):
                rows = slice(D * (h % 2), D * (h % 2) + D)
                dve.wait_ge(s_o_low, b * NH + (h + 1))
                dve.tensor_tensor(o_cat[rows, h // 2, :], pv[rows, :], side[rows, :], ALU.add).then_inc(s_o, 1)

            def run(body):
                for s, (ahead, behind) in enumerate(zip(body.jobs.ahead, body.jobs.behind)):
                    if s == STEPS:
                        add_o(body.b, NH - 1)
                    for job in ahead + behind:
                        do(body, job)
                    if s < STEPS:
                        if s > TT and (s - LAG + 1) % TT == 0:
                            add_o(body.b, (s - LAG + 1) // TT - 1)
                        step_lo(body.b, s)

            dve.memset(ones[:, :], 1.0).then_inc(s_const, 1)
            dve.memset(k_aug[D:D + 1, :, :].bitcast(F32), 1.0).then_inc(s_const, 1)
            dve.memset(side[:, half(1)], 1.0).then_inc(s_bias, 1)
            dve.wait_ge(s_load, NLOAD)
            dve.wait_ge(s_bias, 1)
            for ct in range(CT):
                dve.tensor_scalar(side[:, tile(ct)], side[:, half(1)][:, tile(0)], bv[:, ct:ct + 1], None, ALU.mult
                                  ).then_inc(s_bias, 1)
            dve.wait_ge(s_bias_ps, 1)
            dve.tensor_tensor(bias_all[:, :], pv[:, half(0)], bias_all[:, :], ALU.add).then_inc(s_bias, 1)
            for job in FIRST.ahead[0]:
                do(first, job)
            with dve.Fori(0, BATCH - 1) as b:
                run(looped(b))
            run(last)

        @block.gpsimd
        def _(pool):
            def do(body, s, job):
                kind, b = job[0], body.b
                if kind == "group_var":
                    pool.wait_ge(s_taken[body.bank(job)], body.done(job))
                    pool.tensor_tensor(rstd[:, :], gvar[:, :], power[:, :], ALU.pow).then_inc(s_rstd, 1)
                if kind == "reciprocal_row":
                    h = job[1]
                    rows = slice(D * (h % 2), D * (h % 2) + D)
                    pool.wait_ge(s_sum, b * (NH * NSUM) + NSUM * (s // TT) + s % TT)
                    pool.wait_ge(s_o, b * NH + (h + 1))
                    pool.wait_ge(s_recip_all, b * (16 * NH) + 16 * (h + 1))
                    pool.tensor_tensor(o_cat[rows, h // 2, :], o_cat[rows, h // 2, :], side[rows, :], ALU.mult
                                       ).then_inc(s_o_norm, 1)
                    pool.wait_ge(s_o_norm, b * NH + (h + 1))
                if kind == "out":
                    tt = job[1]
                    pool.wait_ge(s_res[tt % NRES], b * 32 + 16 * (tt // NRES + 1))
                    pool.tensor_tensor(res(tt), res(tt), bias_all[:, :], ALU.add).then_inc(s_res_bias, 1)

            def step_sum(b, s):
                h, kt = s // TT, s % TT
                total = key_sum[:, h % 2, :]
                pool.wait_ge(s_exp, b * STEPS + (s + 1))
                if kt == 1:
                    if h >= 2:
                        pool.wait_ge(s_recip_row, b * (16 * NH) + 16 * (h - 1))
                    pool.tensor_tensor(total, prob[:, 0, :], prob[:, 1, :], ALU.add).then_inc(s_sum, 1)
                else:
                    pool.wait_ge(s_sum, b * (NH * NSUM) + NSUM * h + (kt - 1))
                    pool.tensor_tensor(total, total, prob[:, s % 2, :], ALU.add).then_inc(s_sum, 1)

            def run(body):
                for s, (ahead, behind) in enumerate(zip(body.jobs.ahead, body.jobs.behind)):
                    if s < STEPS and s % TT:
                        step_sum(body.b, s)
                    for job in ahead + behind:
                        do(body, s, job)

            pool.memset(ident[:, :], 0.0).then_inc(s_build, 1)
            pool.memset(group[:, :], 1.0 / GC).then_inc(s_build, 1)
            pool.memset(power[:, :], -0.5).then_inc(s_build, 1)
            pool.wait_ge(s_build, 3)
            pool.affine_select(out=ident[:, :], in_=ident[:, :], compare_op=ALU.not_equal, fill=1.0, base=0,
                               pattern=[[-1, P]], channel_multiplier=1).then_inc(s_const, 1)
            blocks = group[:, :].rearrange("p (g c) -> p g c", c=GC)
            pool.affine_select(out=blocks, in_=blocks, compare_op=ALU.is_ge, fill=0.0, base=0,
                               pattern=[[-GC, P // GC], [0, GC]], channel_multiplier=1).then_inc(s_build, 1)
            pool.wait_ge(s_build, 4)
            pool.affine_select(out=blocks, in_=blocks, compare_op=ALU.is_ge, fill=0.0, base=GC - 1,
                               pattern=[[GC, P // GC], [0, GC]], channel_multiplier=-1).then_inc(s_const, 1)
            pool.wait_ge(s_bias, 6)
            for job in FIRST.ahead[0]:
                do(first, 0, job)
            with pool.Fori(0, BATCH - 1) as b:
                run(looped(b))
            run(last)


_INS = {"x": "x", "L0_conv_gamma": "gamma", "L0_conv_beta": "beta", "L0_conv_w_qkv": "w_qkv",
        "L0_conv_b_qkv": "b_qkv", "L0_conv_w_out": "w_out", "L0_conv_b_out": "b_out"}


def kernel(**inputs):
    import numpy as np
    import concourse.bacc as bacc
    from concourse.bass_utils import run_bass_kernel_spmd

    nc = bacc.Bacc("TRN2", target_bir_lowering=False, num_devices=1)
    arrays, args = {}, {}
    for name, arg in _INS.items():
        a = np.ascontiguousarray(inputs[name])
        arrays[f"in_{arg}"] = a
        args[arg] = nc.dram_tensor(f"in_{arg}", a.shape, mybir.dt.from_np(a.dtype), kind="ExternalInput").ap()
    out = nc.dram_tensor("out_0", (BATCH, HH, WW, C), F32, kind="ExternalOutput").ap()
    build(nc, out=out, **args)
    r = run_bass_kernel_spmd(nc, [arrays], core_ids=[0])
    return r.results[0]["out_0"]
```

```python
from contextlib import ExitStack

import concourse.bass as bass
from concourse import mybir

F32 = mybir.dt.float32
F32R = mybir.dt.float32r
ALU = mybir.AluOpType
ACT = mybir.ActivationFunctionType
AX_X = mybir.AxisListType.X

P = 128
BATCH, HH, WW, C = 16, 32, 32, 512
L = HH * WW
D = 64
NH = C // D
NPAIR = NH // 2
CT = C // P
TT = L // P
HALF = 512
NHALF = L // HALF
GROUPS = 32
GC = C // GROUPS
EPS = 1e-5
SCALE = 1.0 / 8.0
STEPS = NH * TT
LAG = 2
NSLOT = 4
NRES = 4
QK_ITEMS = 2 * NHALF


PV_COST, PART_COST = 0.9, 0.86
COST = {"x": 0.5, "group_mean": 0.1, "group_var": 0.1, "qk": 0.86, "v": 3.5, "max": 0.2, "max_row": 0.2,
        "denominator": 1.8, "reciprocal_row": 0.2, "out": 3.5}
READ = {"x": 0.8, "group_mean": 0.3, "group_var": 0.3, "qk": 3.5, "v": 1.5, "max": 0.8, "max_row": 0.4,
        "denominator": 0.4, "reciprocal_row": 0.4, "out": 0.8}
NO_BANK = ("qk_part", "statistics", "scale", "normalize")


def of_next(job):
    kind, n = job[0], job[1]
    return kind in ("qk", "qk_part") and (n == 0 or job[1:4] in EARLY) or kind in ("max", "max_row") and n < 2


EARLY = [(1, 0, 0)]


def whole_qk(job):
    return [("qk_part", *job, ct) for ct in range(CT - 1)] + [("qk", *job)]


def schedule(prepare_next):
    ahead = [[] for _ in range(STEPS + 1)]
    behind = [[] for _ in range(STEPS + 1)]

    def project(jobs, start):
        for i, job in enumerate(jobs):
            entries = whole_qk(job)
            behind[start + 2 * i] += entries[:2]
            behind[start + 2 * i + 1] += entries[2:]

    def maxima(h, steps):
        for qt, s in enumerate(steps):
            ahead[s].append(("max", h, qt, 0))
            behind[s].insert(0, ("max", h, qt, 1))

    def qk_jobs(pair):
        return [(pair, i // NHALF, i % NHALF) for i in range(QK_ITEMS)]

    for pair in range(1, NPAIR):
        jobs = [job for job in qk_jobs(pair) if job not in EARLY]
        project(jobs, 0 if pair == 1 else 16 * pair - 18)
    if prepare_next:
        for tt in range(TT):
            behind[38 + tt].append(("x", tt))
        for i in range(CT):
            behind[38 + TT // 2 + i].append(("statistics", i, 0))
        for i in range(CT):
            behind[38 + TT + i // 2].append(("statistics", i, 1))
        behind[48].append(("group_mean",))
        behind[49].append(("group_var",))
        behind[50].append(("scale",))
        for i in range(CT):
            behind[50 + i // 2].append(("normalize", i))
        project(qk_jobs(0), 51)
        maxima(0, range(59, 64))
    for h in range(2, NH):
        at = 8 * (h - 1) - 2
        maxima(h, range(at, at + 8))
        behind[at + 8].append(("max_row", h))
    for h in range(NH - 1):
        behind[8 * h + 9].append(("denominator", h))
        behind[8 * h + 10].append(("reciprocal_row", h))
    tail = ahead[STEPS]
    if prepare_next:
        max0 = [("max", 0, qt, i) for qt in range(5, TT) for i in range(NHALF)]
        max1 = [("max", 1, qt, i) for qt in range(TT) for i in range(NHALF)]
        tail += [("v", 0), *max0[:2], ("v", 1), ("denominator", NH - 1), *max0[2:4], ("v", 2)]
        tail += [("reciprocal_row", NH - 1), *max0[4:], *whole_qk(EARLY[0]), ("max_row", 0)]
        for tt in range(TT):
            tail += [("out", tt), *max1[2 * tt:2 * tt + 2]]
        tail += [("v", 3), ("max_row", 1)] + [("v", tt) for tt in range(4, TT)]
    else:
        tail += [("denominator", NH - 1), ("reciprocal_row", NH - 1)] + [("out", tt) for tt in range(TT)]
    return ahead, behind


def first_schedule():
    jobs = [("x", tt) for tt in range(TT)] + [("statistics", ct, i) for i in range(NHALF) for ct in range(CT)]
    jobs += [("group_mean",), ("group_var",), ("scale",)] + [("normalize", ct) for ct in range(CT)]
    for i in range(QK_ITEMS):
        jobs += whole_qk((0, i // NHALF, i % NHALF))
    jobs += [("max", 0, qt, half) for qt in range(TT) for half in range(NHALF)] + [("max_row", 0)]
    for job in EARLY:
        jobs += whole_qk(job)
    jobs += [("max", 1, qt, half) for qt in range(TT) for half in range(NHALF)] + [("max_row", 1)]
    return [jobs + [("v", tt) for tt in range(TT)]], [[]]


class Jobs:

    def __init__(self, schedule):
        self.ahead, self.behind = schedule
        self.bank, self.no, self.total = {}, {}, [0, 0]
        now, free, held = 0.0, [0.0, 0.0], None
        for a, b in zip(self.ahead, self.behind):
            now += PV_COST
            for n, job in enumerate(a + b):
                if n == len(a):
                    now += PV_COST
                part = job[0] == "qk_part"
                whole = ("qk", *job[1:4]) if part else job
                if job[0] in NO_BANK and not part:
                    continue
                if whole not in self.bank:
                    bank = 0 if free[0] <= free[1] else 1
                    if held is not None:
                        bank = 1 - held
                    self.bank[whole], self.no[whole] = bank, self.total[bank]
                    self.total[bank] += 1
                bank = self.bank[whole]
                now = max(now, free[bank]) + (PART_COST if part else COST[job[0]])
                if job[0] in ("qk", "qk_part"):
                    held = bank if part else None
                if not part:
                    free[bank] = now + READ[job[0]]


FIRST = Jobs(first_schedule())
LOOP = Jobs(schedule(True))
LAST = Jobs(schedule(False))


class Body:

    def __init__(self, b, prepares, jobs, loops):
        self.b = b
        self.prepares = prepares
        self.jobs, self.loops = jobs, loops

    def bank(self, job):
        return self.jobs.bank[("qk", *job[1:4]) if job[0] == "qk_part" else job]

    def before(self, bank):
        return 0 if self.loops is None else self.loops * LOOP.total[bank] + FIRST.total[bank]

    def free(self, job):
        return self.before(self.bank(job)) + self.jobs.no[job]

    def done(self, job):
        return self.before(self.bank(job)) + (self.jobs.no[job] + 1)


def build(nc, x, gamma, beta, w_qkv, b_qkv, w_out, b_out, out):
    x_flat = x.rearrange("b h w c -> (b h w c)")
    out_flat = out.rearrange("b h w c -> (b h w c)")

    with ExitStack() as ctx:
        def sb(name, shape, dt=F32):
            return ctx.enter_context(nc.sbuf_tensor(name, shape, dt))

        def ps(name, shape):
            return ctx.enter_context(nc.psum_tensor(name, shape, F32))

        def sem(name):
            return ctx.enter_context(nc.semaphore(name))

        wqkv = sb("wqkv", [P, CT, 3 * C])
        wout = sb("wout", [P, CT, C])
        ident = sb("ident", [P, P])
        group = sb("group", [P, P])
        ones = sb("ones", [P, 2])
        bias_all = sb("bias_all", [P, C])
        bv = sb("bv", [P, CT])
        gamma_c = sb("gamma_c", [P, CT])
        beta_c = sb("beta_c", [P, CT])
        bqk = sb("bqk", [P, 2, NPAIR])
        bqk_odd = sb("bqk_odd", [D, 2, NPAIR])
        xt = sb("xt", [P, 2, C])
        xn = sb("xn", [P, CT, L])
        bn = sb("bn", [P, CT, NHALF, 6])
        carrier = sb("carrier", [P, 1])
        chan = sb("chan", [P, CT, 2])
        grp = sb("grp", [P, CT, 2])
        dev = sb("dev", [P, CT])
        dev2 = sb("dev2", [P, CT])
        gvar = sb("gvar", [P, CT])
        power = sb("power", [P, CT])
        rstd = sb("rstd", [P, CT])
        mul = sb("mul", [P, CT])
        off = sb("off", [P, CT])
        moff = sb("moff", [P, CT])
        k_stack = sb("k_stack", [P, NSLOT, L], F32R)
        k_aug = sb("k_aug", [D + 1, NSLOT, L], F32R)
        q_twin = sb("q_twin", [P, NSLOT, L], F32R)
        q_aug = sb("q_aug", [D + 1, NSLOT, L], F32R)
        v_stack = sb("v_stack", [P, TT, NPAIR, 4, D], F32R)
        mx = sb("mx", [P, TT, NHALF])
        mrow = sb("mrow", [P, TT])
        neg_max = sb("neg_max", [TT, P], F32R)
        prob = sb("prob", [P, 2, L])
        prob_hi = sb("prob_hi", [P, 2, L], F32R)
        prob_lo = sb("prob_lo", [P, 2, L], F32R)
        key_sum = sb("key_sum", [P, 2, L])
        recip = sb("recip", [P, TT])
        recip_t = sb("recip_t", [TT, P])
        side = sb("side", [P, L])
        o_cat = sb("o_cat", [P, NPAIR, L])

        recip_dram = nc.dram_tensor("recip_dram", [2, TT, P], F32, kind="Internal").ap()

        def res(tt):
            return prob[:, (tt % NRES) // 2, (tt % 2) * HALF:(tt % 2 + 1) * HALF]

        scores = ps("scores", [P, 2, L])
        pv = ps("pv", [P, L])
        spare = ps("spare", [P, 2, HALF])

        s_build = sem("s_build")
        s_load = sem("s_load")
        s_const = sem("s_const")
        s_x_load = [sem(f"s_x_load{i}") for i in range(2)]
        s_stat = sem("s_stat")
        s_rstd = sem("s_rstd")
        s_xn = sem("s_xn")
        s_filled = [sem(f"s_filled{i}") for i in range(2)]
        s_taken = [sem(f"s_taken{i}") for i in range(2)]
        s_qk_hi = sem("s_qk_hi")
        s_second_hi = sem("s_second_hi")
        s_v_hi = sem("s_v_hi")
        s_bias = sem("s_bias")
        s_bias_ps = sem("s_bias_ps")
        s_rowmax = sem("s_rowmax")
        s_shift = sem("s_shift")
        s_scores = sem("s_scores")
        s_exp = sem("s_exp")
        s_hi = sem("s_hi")
        s_lo = sem("s_lo")
        s_sum = sem("s_sum")
        s_pv = sem("s_pv")
        s_o_low = sem("s_o_low")
        s_o = sem("s_o")
        s_recip_row = sem("s_recip_row")
        s_recip_all = [sem(f"s_recip_all{i}") for i in range(2)]
        s_o_norm = sem("s_o_norm")
        s_res = [sem(f"s_res{i}") for i in range(NRES)]
        s_res_bias = sem("s_res_bias")
        s_store = [sem(f"s_store{i}") for i in range(NRES)]

        NLOAD = 16 * (2 * CT + 2 + 2 * 2 + 2)
        NCONST = 4
        NSTAT = 7
        NSUM = TT - 1

        first = Body(None, 0, FIRST, None)
        last = Body(BATCH - 1, None, LAST, BATCH - 1)

        def looped(b):
            return Body(b, b + 1, LOOP, b)

        def half(i):
            return slice(i * HALF, (i + 1) * HALF)

        def tile(i):
            return slice(i * P, (i + 1) * P)

        def tokens(dram, start):
            return dram[bass.ds(start, P * C)].rearrange("(p c) -> p c", c=C)

        def image_of(body, job):
            return body.prepares if of_next(job) else body.b

        def last_of_banks(body, jobs):
            return [[job for job in jobs if body.bank(job) == i][-1] for i in range(2)
                    if any(body.bank(job) == i for job in jobs)]

        def qk_hi_value(body, job):
            _, pair, which, i = job
            return image_of(body, job) * (NPAIR * QK_ITEMS) + (QK_ITEMS * pair + which * NHALF + i + 1)

        def divided_at(s):
            return s // TT - 2 if s % TT == 0 and s >= 2 * TT else None

        block = ctx.enter_context(nc.Block())

        @block.sync
        def _(sp):
            def early(value):
                return value if isinstance(value, int) else sp.snap(value)

            def start_of(n, tt):
                return early(n * (L * C) + tt * P * C)

            def load_x(body, tt):
                n = body.prepares
                start = start_of(n, tt)
                if tt >= 2:
                    job = ("x", tt - 2)
                    sp.wait_ge(s_taken[body.bank(job)], body.done(job))
                elif body is not first:
                    sp.wait_ge(s_v_hi, n * TT)
                sp.dma_start(xt[:, tt % 2, :], tokens(x_flat, start)).then_inc(s_x_load[tt % 2], 16)

            def second_hi(body, job):
                _, pair, which, i = job
                slots = slice(2 * pair % NSLOT, 2 * pair % NSLOT + 2)
                sp.wait_ge(s_qk_hi, qk_hi_value(body, job))
                sp.dma_start((q_twin[D:P, slots, half(i)], k_aug[0:D, slots, half(i)])[which].bitcast(F32),
                             (q_twin, k_stack)[which][0:D, slots, half(i)].bitcast(F32)).then_inc(s_second_hi, 16)

            def shift_row(body, job):
                h = job[1]
                sp.wait_ge(s_taken[body.bank(job)], body.done(job))
                sp.dma_start(q_aug[D:D + 1, h % NSLOT, :].bitcast(F32).rearrange("a (t p) -> a t p", p=P),
                             neg_max[:, :].bitcast(F32)
                             ).then_inc(s_shift, 16)

            def recip_rows(body, job):
                h = job[1]
                rows = slice(D * (h % 2), D * (h % 2) + D)
                sp.wait_ge(s_taken[body.bank(job)], body.done(job))
                sp.dma_start(recip_dram[h % 2, :, :], recip_t[:, :]).then_inc(s_recip_row, 16)
                sp.wait_ge(s_recip_row, body.b * (16 * NH) + 16 * (h + 1))
                sp.dma_start(side[rows, :],
                             recip_dram[h % 2, :, :].rearrange("(a t) p -> a (t p)", a=1).broadcast_to([D, L])
                             ).then_inc(s_recip_all[h % 2], 16)

            def load_res(body, tt):
                b = body.b
                start = start_of(b, tt)
                if tt < NRES:
                    steps = early(b * STEPS + STEPS)
                    sums = early(b * (NH * NSUM) + NH * NSUM)
                    sp.wait_ge(s_hi, steps)
                    sp.wait_ge(s_lo, steps)
                    sp.wait_ge(s_sum, sums)
                else:
                    sp.wait_ge(s_store[tt % NRES], b * 32 + 16)
                sp.dma_start(res(tt), tokens(x_flat, start)).then_inc(s_res[tt % NRES], 16)

            def store(body, job):
                tt = job[1]
                start = start_of(body.b, tt)
                sp.wait_ge(s_taken[body.bank(job)], body.done(job))
                sp.dma_start(tokens(out_flat, start), res(tt)).then_inc(s_store[tt % NRES], 16)

            def run(body):
                if body is not last:
                    load_x(body, 0)
                    load_x(body, 1)
                for s, (ahead, behind) in enumerate(zip(body.jobs.ahead, body.jobs.behind)):
                    if s == STEPS:
                        for tt in range(NRES):
                            load_res(body, tt)
                    for job in ahead + behind:
                        if job[0] == "x" and job[1] + 2 < TT:
                            load_x(body, job[1] + 2)
                        if job[0] == "qk":
                            second_hi(body, job)
                        if job[0] == "max_row":
                            shift_row(body, job)
                        if job[0] == "reciprocal_row":
                            recip_rows(body, job)
                        if job[0] == "out":
                            store(body, job)
                            if job[1] + NRES < TT:
                                load_res(body, job[1] + NRES)

            for ct in range(CT):
                sp.dma_start(wqkv[:, ct, :], w_qkv[tile(ct), :]).then_inc(s_load, 16)
                sp.dma_start(wout[:, ct, :], w_out[tile(ct), :]).then_inc(s_load, 16)
            with nc.allow_non_contiguous_dma("a few small vectors, once"):
                sp.dma_start(gamma_c[:, :], gamma.rearrange("(t p) -> p t", p=P)).then_inc(s_load, 16)
                sp.dma_start(beta_c[:, :], beta.rearrange("(t p) -> p t", p=P)).then_inc(s_load, 16)
                sp.dma_start(bv[:, :], b_qkv[2 * C:3 * C].rearrange("(t p) -> p t", p=P)).then_inc(s_load, 16)
                for j in range(2):
                    part = b_qkv[j * C:(j + 1) * C].rearrange("(t p) -> p t", p=P)
                    sp.dma_start(bqk[:, j, :], part).then_inc(s_load, 16)
                    sp.dma_start(bqk_odd[:, j, :], part[D:P, :]).then_inc(s_load, 16)
            sp.dma_start(bias_all[:, :], b_out.rearrange("(a c) -> a c", a=1).broadcast_to([P, C])
                         ).then_inc(s_load, 16)
            run(first)
            with sp.Fori(0, BATCH - 1) as b:
                run(looped(b))
            run(last)
            for i in range(NRES):
                sp.wait_ge(s_store[i], BATCH * 32)

        @block.tensor
        def _(pe):
            def project(job, bank, ct):
                pair, which, i = job[1:4]
                return pe.matmul(bank, wqkv[:, ct, which * C + pair * P:which * C + (pair + 1) * P],
                                 xn[:, ct, half(i)], start=(ct == 0), stop=(ct == CT - 1), skip_group_check=True)

            def do(body, job):
                kind = job[0]
                if kind in NO_BANK and kind != "qk_part":
                    return
                if kind == "qk_part":
                    whole = ("qk", *job[1:4])
                    bank = spare[:, body.bank(whole), :]
                    if job[4] == 0:
                        if not (body is first and body.jobs.no[whole] == 0):
                            pe.wait_ge(s_taken[body.bank(whole)], body.free(whole))
                        if job[1] == 0:
                            pe.wait_ge(s_xn, body.prepares * CT + CT)
                    project(whole, bank, job[4])
                    return
                if kind == "qk":
                    project(job, spare[:, body.bank(job), :], CT - 1).then_inc(s_filled[body.bank(job)], 1)
                    return
                bank = spare[:, body.bank(job), :]
                if not (body is first and body.jobs.no[job] == 0):
                    pe.wait_ge(s_taken[body.bank(job)], body.free(job))
                if kind == "x":
                    tt = job[1]
                    pe.wait_ge(s_x_load[tt % 2], body.prepares * (8 * TT) + 16 * (tt // 2 + 1))
                    for ct in range(CT):
                        mm = pe.transpose(bank[:, tile(ct)], xt[:, tt % 2, tile(ct)], ident[:, :])
                elif kind == "group_mean":
                    pe.wait_ge(s_stat, body.prepares * NSTAT + 2)
                    mm = pe.matmul(bank[:, 0:2 * CT], group[:, :], chan[:, :, :].rearrange("p t s -> p (t s)"),
                                   start=True, stop=True)
                elif kind == "group_var":
                    pe.wait_ge(s_stat, body.prepares * NSTAT + 4)
                    mm = pe.matmul(bank[:, 0:CT], group[:, :], dev2[:, :], start=True, stop=True)
                elif kind == "v":
                    for ct in range(CT):
                        mm = pe.matmul(bank, xn[:, ct, tile(job[1])], wqkv[:, ct, 2 * C:3 * C],
                                       start=(ct == 0), stop=(ct == CT - 1))
                elif kind == "max":
                    _, h, qt, i = job
                    if h % 2 == 0 and qt == 0 and i == 0:
                        made = [("qk", h // 2, which, j) for which in range(2) for j in range(NHALF)
                                if (h // 2, which, j) not in EARLY]
                        other = [j for j in made if body.bank(j) != body.bank(job)]
                        if other:
                            pe.wait_ge(s_taken[body.bank(other[-1])], body.done(other[-1]))
                        pe.wait_ge(s_second_hi, (image_of(body, job) * NPAIR + (h // 2 + 1)) * (16 * QK_ITEMS))
                    mm = pe.matmul(bank, q_twin[:, h % NSLOT, tile(qt)], k_stack[:, h % NSLOT, half(i)],
                                   start=True, stop=True)
                elif kind == "max_row":
                    h = job[1]
                    pe.wait_ge(s_rowmax, image_of(body, job) * NH + (h + 1))
                    mm = pe.transpose(bank[0:TT, 0:P], mrow[:, :], ident[:, :])
                elif kind == "denominator":
                    h = job[1]
                    pe.wait_ge(s_sum, body.b * (NH * NSUM) + NSUM * (h + 1))
                    for qt in range(TT):
                        mm = pe.matmul(bank[:, qt:qt + 1], key_sum[:, h % 2, tile(qt)], ones[:, 0:1],
                                       start=True, stop=True)
                elif kind == "reciprocal_row":
                    pe.wait_ge(s_o, body.b * NH + (job[1] + 1))
                    made = ("denominator", job[1])
                    if body.bank(made) != body.bank(job):
                        pe.wait_ge(s_taken[body.bank(made)], body.done(made))
                    mm = pe.transpose(bank[0:TT, 0:P], recip[:, :], ident[:, :])
                elif kind == "out":
                    if job[1] == 0:
                        pe.wait_ge(s_o_norm, body.b * NH + NH)
                    for ct in range(CT):
                        mm = pe.matmul(bank, o_cat[:, ct, tile(job[1])], wout[:, ct, :],
                                       start=(ct == 0), stop=(ct == CT - 1))
                mm.then_inc(s_filled[body.bank(job)], 1)

            def step_scores(b, s):
                h, kt = s // TT, s % TT
                slot = h % NSLOT
                if kt == 0:
                    pe.wait_ge(s_shift, b * (16 * NH) + 16 * (h + 1))
                if s >= 2:
                    pe.wait_ge(s_exp, b * STEPS + (s - 1))
                for i in range(NHALF):
                    pe.matmul(scores[:, s % 2, half(i)], k_stack[:, slot, tile(kt)], q_twin[:, slot, half(i)],
                              start=True, stop=False)
                for i in range(NHALF):
                    mm = pe.matmul(scores[:, s % 2, half(i)], k_aug[:, slot, tile(kt)], q_aug[:, slot, half(i)],
                                   start=False, stop=True)
                mm.then_inc(s_scores, 1)

            def step_pv(b, s):
                h, kt = s // TT, s % TT
                if kt == 0 and h > 0:
                    pe.wait_ge(s_o, b * NH + h)
                v = v_stack[:, kt, h // 2, 2 * (h % 2):2 * (h % 2) + 2, :].rearrange("p a d -> p (a d)")
                pe.wait_ge(s_hi, b * STEPS + (s + 1))
                for i in range(NHALF):
                    pe.matmul(pv[:, half(i)], v, prob_hi[:, s % 2, half(i)], start=(kt == 0), stop=False)
                pe.wait_ge(s_lo, b * STEPS + (s + 1))
                for i in range(NHALF):
                    mm = pe.matmul(pv[:, half(i)], v, prob_lo[:, s % 2, half(i)], start=False,
                                   stop=(kt == TT - 1))
                mm.then_inc(s_pv, 1)

            def run(body):
                for bank in range(2):
                    pe.wait_ge(s_taken[bank], body.before(bank))
                for s, (ahead, behind) in enumerate(zip(body.jobs.ahead, body.jobs.behind)):
                    if s < STEPS:
                        step_scores(body.b, s)
                    if s == STEPS:
                        pe.wait_ge(s_exp, body.b * STEPS + STEPS)
                    for n, job in enumerate(ahead):
                        if s == STEPS and n < LAG:
                            step_pv(body.b, s - LAG + n)
                        do(body, job)
                    if LAG <= s < STEPS:
                        step_pv(body.b, s - LAG)
                    for job in behind:
                        do(body, job)

            pe.wait_ge(s_load, NLOAD)
            pe.wait_ge(s_const, NCONST)
            pe.wait_ge(s_bias, 5)
            for ct in range(CT):
                mm = pe.matmul(pv[:, half(0)], side[:, tile(ct)], wout[:, ct, :],
                               start=(ct == 0), stop=(ct == CT - 1))
            mm.then_inc(s_bias_ps, 1)
            for job in FIRST.ahead[0]:
                do(first, job)
            with pe.Fori(0, BATCH - 1) as b:
                run(looped(b))
            run(last)

        @block.scalar
        def _(act):
            def do(body, job):
                kind = job[0]
                if kind in NO_BANK:
                    return
                bank = spare[:, body.bank(job), :]
                taken = s_taken[body.bank(job)]
                if kind in ("x", "qk", "v", "max_row", "reciprocal_row"):
                    act.wait_ge(s_filled[body.bank(job)], body.done(job))
                if kind == "x":
                    act.activation(xn[:, :, tile(job[1])], bank.rearrange("p (t c) -> p t c", t=CT), ACT.Copy
                                   ).then_inc(taken, 1)
                if kind == "qk":
                    _, pair, which, i = job
                    for e in range(2):
                        rows = slice(D * e, D * e + D)
                        hi = act.activation((q_twin, k_stack)[which][0:D, (2 * pair + e) % NSLOT, half(i)],
                                            bank[rows, :], ACT.Identity, bias=bqk[rows, which, pair:pair + 1])
                    hi.then_inc(s_qk_hi, 1)
                if kind == "v":
                    act.activation(v_stack[:, job[1], :, 0::3, :],
                                   bank.rearrange("p (a e d) -> p a e d", e=2, d=D), ACT.Copy).then_inc(s_v_hi, 1)
                if kind == "max_row":
                    h = job[1]
                    if not (body is first and h == 0):
                        act.wait_ge(s_shift, image_of(body, job) * (16 * NH) + 16 * h)
                    act.activation(neg_max[:, :], bank[0:TT, 0:P], ACT.Copy, scale=-1.0).then_inc(taken, 1)
                if kind == "reciprocal_row":
                    if job[1] > 0:
                        act.wait_ge(s_recip_row, body.b * (16 * NH) + 16 * job[1])
                    act.activation(recip_t[:, :], bank[0:TT, 0:P], ACT.Copy).then_inc(taken, 1)

            def step_exp(b, s):
                act.wait_ge(s_scores, b * STEPS + (s + 1))
                if s >= 2:
                    h, kt = (s - 2) // TT, (s - 2) % TT
                    act.wait_ge(s_lo, b * STEPS + (s - 1))
                    act.wait_ge(s_sum, b * (NH * NSUM) + NSUM * h + max(kt, 1))
                act.activation(prob[:, s % 2, :], scores[:, s % 2, :], ACT.Exp, scale=SCALE).then_inc(s_exp, 1)

            def step_hi(b, s):
                act.wait_ge(s_exp, b * STEPS + (s + 1))
                if s >= 2:
                    act.wait_ge(s_pv, b * STEPS + (s - 1))
                act.activation(prob_hi[:, s % 2, :], prob[:, s % 2, :], ACT.Copy).then_inc(s_hi, 1)

            def take_o_low(b, h):
                act.wait_ge(s_pv, b * STEPS + TT * (h + 1))
                if h >= 2:
                    act.wait_ge(s_o_norm, b * NH + (h - 1))
                to, frm = D * (h % 2), D * (1 - h % 2)
                act.activation(side[to:to + D, :], pv[frm:frm + D, :], ACT.Copy).then_inc(s_o_low, 1)

            def run(body):
                for s, (ahead, behind) in enumerate(zip(body.jobs.ahead, body.jobs.behind)):
                    if s < STEPS:
                        step_exp(body.b, s)
                        if s > TT and (s - LAG + 1) % TT == 0:
                            take_o_low(body.b, (s - LAG + 1) // TT - 1)
                        step_hi(body.b, s)
                    else:
                        take_o_low(body.b, NH - 1)
                    for job in ahead + behind:
                        do(body, job)
                if body is not last:
                    for i in range(NRES):
                        act.wait_ge(s_store[i], body.b * 32 + 32)

            act.wait_ge(s_load, NLOAD)
            for job in FIRST.ahead[0]:
                do(first, job)
            with act.Fori(0, BATCH - 1) as b:
                run(looped(b))
            run(last)

        @block.vector
        def _(dve):
            def do(body, job):
                kind, n = job[0], body.prepares
                if kind not in NO_BANK:
                    bank = spare[:, body.bank(job), :]
                    taken = s_taken[body.bank(job)]
                if kind in ("group_mean", "group_var", "max", "denominator", "out"):
                    dve.wait_ge(s_filled[body.bank(job)], body.done(job))
                if kind == "statistics":
                    _, ct, i = job
                    if ct == 0:
                        tiles = [("x", tt) for tt in range(i * TT // 2, (i + 1) * TT // 2)]
                        for x_job in last_of_banks(body, tiles):
                            dve.wait_ge(s_taken[body.bank(x_job)], body.done(x_job))
                    a = dve.bn_stats(bn[:, ct, i, :], xn[:, ct, half(i)])
                    if ct == CT - 1 and i == NHALF - 1:
                        a.then_inc(s_stat, 1)
                        dve.wait_ge(s_stat, n * NSTAT + 1)
                        dve.memset(carrier[:, :], 0.0)
                        for j in range(CT):
                            a = dve.bn_aggr(chan[:, j, :], bn[:, j, :, :])
                        a.then_inc(s_stat, 1)
                if kind == "group_mean":
                    dve.tensor_copy(grp[:, :, :].rearrange("p t s -> p (t s)"), bank[:, 0:2 * CT]).then_inc(taken, 1)
                    dve.wait_ge(taken, body.done(job))
                    dve.tensor_tensor(dev[:, :], chan[:, :, 0], grp[:, :, 0], ALU.subtract).then_inc(s_stat, 1)
                    dve.wait_ge(s_stat, n * NSTAT + 3)
                    dve.tensor_tensor(dev2[:, :], dev[:, :], dev[:, :], ALU.mult).then_inc(s_stat, 1)
                if kind == "group_var":
                    dve.scalar_tensor_tensor(out=gvar[:, :], in0=bank[:, 0:CT], scalar=EPS, in1=grp[:, :, 1],
                                             op0=ALU.add, op1=ALU.add).then_inc(taken, 1)
                if kind == "scale":
                    dve.wait_ge(s_rstd, n + 1)
                    dve.tensor_tensor(mul[:, :], rstd[:, :], gamma_c[:, :], ALU.mult).then_inc(s_stat, 1)
                    dve.wait_ge(s_stat, n * NSTAT + 5)
                    dve.tensor_tensor(moff[:, :], grp[:, :, 0], mul[:, :], ALU.mult).then_inc(s_stat, 1)
                    dve.wait_ge(s_stat, n * NSTAT + 6)
                    dve.tensor_tensor(off[:, :], beta_c[:, :], moff[:, :], ALU.subtract).then_inc(s_stat, 1)
                if kind == "normalize":
                    ct = job[1]
                    if ct == 0:
                        dve.wait_ge(s_stat, n * NSTAT + 7)
                    dve.tensor_scalar(xn[:, ct, :], xn[:, ct, :], mul[:, ct:ct + 1], off[:, ct:ct + 1],
                                      ALU.mult, ALU.add).then_inc(s_xn, 1)
                if kind == "qk":
                    _, pair, which, i = job
                    dve.wait_ge(s_qk_hi, qk_hi_value(body, job))
                    for e in range(2):
                        slot = (2 * pair + e) % NSLOT
                        hi = (q_twin, k_stack)[which][0:D, slot, half(i)]
                        lo = (q_aug[0:D, slot, half(i)], k_stack[D:P, slot, half(i)])[which]
                        a = dve.scalar_tensor_tensor(out=lo, in0=bank[D * e:D * e + D, :],
                                                     scalar=(bqk, bqk_odd)[e][0:D, which, pair:pair + 1], in1=hi,
                                                     op0=ALU.add, op1=ALU.subtract)
                    a.then_inc(taken, 1)
                if kind == "v":
                    tt = job[1]
                    dve.wait_ge(s_v_hi, n * TT + (tt + 1))
                    dve.tensor_tensor(v_stack[:, tt, :, 1:3, :], bank.rearrange("p (a e d) -> p a e d", e=2, d=D),
                                      v_stack[:, tt, :, 0::3, :], ALU.subtract).then_inc(taken, 1)
                if kind == "max":
                    _, h, qt, i = job
                    if qt == 0 and i == 0 and not (body is first and h == 0):
                        dve.wait_ge(s_rowmax, image_of(body, job) * NH + h)
                    dve.tensor_reduce(mx[:, qt, i:i + 1], bank, AX_X, ALU.max).then_inc(taken, 1)
                    if qt == TT - 1 and i == NHALF - 1:
                        for end in last_of_banks(body, [("max", h, j // NHALF, j % NHALF)
                                                        for j in range(TT * NHALF)]):
                            dve.wait_ge(s_taken[body.bank(end)], body.done(end))
                        dve.tensor_tensor(mrow[:, :], mx[:, :, 0], mx[:, :, 1], ALU.max).then_inc(s_rowmax, 1)
                if kind == "denominator":
                    dve.reciprocal(recip[:, :], bank[:, 0:TT]).then_inc(taken, 1)
                if kind == "out":
                    tt = job[1]
                    dve.wait_ge(s_res_bias, body.b * TT + (tt + 1))
                    dve.tensor_tensor(res(tt), bank, res(tt), ALU.add).then_inc(taken, 1)

            def step_lo(b, s):
                dve.wait_ge(s_hi, b * STEPS + (s + 1))
                if s >= 2:
                    dve.wait_ge(s_pv, b * STEPS + (s - 1))
                dve.tensor_tensor(prob_lo[:, s % 2, :], prob[:, s % 2, :], prob_hi[:, s % 2, :], ALU.subtract
                                  ).then_inc(s_lo, 1)

            def add_o(b, h):
                rows = slice(D * (h % 2), D * (h % 2) + D)
                dve.wait_ge(s_o_low, b * NH + (h + 1))
                dve.tensor_tensor(o_cat[rows, h // 2, :], pv[rows, :], side[rows, :], ALU.add).then_inc(s_o, 1)

            def run(body):
                for s, (ahead, behind) in enumerate(zip(body.jobs.ahead, body.jobs.behind)):
                    if s == STEPS:
                        add_o(body.b, NH - 1)
                        for job in ahead:
                            do(body, job)
                        break
                    for job in ahead + behind:
                        if job[0] == "max":
                            do(body, job)
                    if s < STEPS:
                        if s > TT and (s - LAG + 1) % TT == 0:
                            add_o(body.b, (s - LAG + 1) // TT - 1)
                        step_lo(body.b, s)
                    for job in ahead + behind:
                        if job[0] != "max":
                            do(body, job)

            dve.memset(ones[:, :], 1.0).then_inc(s_const, 1)
            dve.memset(k_aug[D:D + 1, :, :].bitcast(F32), 1.0).then_inc(s_const, 1)
            dve.memset(side[:, half(1)], 1.0).then_inc(s_bias, 1)
            dve.wait_ge(s_load, NLOAD)
            dve.wait_ge(s_bias, 1)
            for ct in range(CT):
                dve.tensor_scalar(side[:, tile(ct)], side[:, half(1)][:, tile(0)], bv[:, ct:ct + 1], None, ALU.mult
                                  ).then_inc(s_bias, 1)
            dve.wait_ge(s_bias_ps, 1)
            dve.tensor_tensor(bias_all[:, :], pv[:, half(0)], bias_all[:, :], ALU.add).then_inc(s_bias, 1)
            for job in FIRST.ahead[0]:
                do(first, job)
            with dve.Fori(0, BATCH - 1) as b:
                run(looped(b))
            run(last)

        @block.gpsimd
        def _(pool):
            def do(body, s, job):
                kind, b = job[0], body.b
                if kind == "group_var":
                    pool.wait_ge(s_taken[body.bank(job)], body.done(job))
                    pool.tensor_tensor(rstd[:, :], gvar[:, :], power[:, :], ALU.pow).then_inc(s_rstd, 1)
                if kind == "reciprocal_row" and job[1] == NH - 1:
                    divide(b, s, NH - 1)
                if kind == "out":
                    tt = job[1]
                    pool.wait_ge(s_res[tt % NRES], b * 32 + 16 * (tt // NRES + 1))
                    pool.tensor_tensor(res(tt), res(tt), bias_all[:, :], ALU.add).then_inc(s_res_bias, 1)

            def divide(b, s, h):
                rows = slice(D * (h % 2), D * (h % 2) + D)
                pool.wait_ge(s_sum, b * (NH * NSUM) + NSUM * (s // TT) + s % TT)
                pool.wait_ge(s_o, b * NH + (h + 1))
                pool.wait_ge(s_recip_all[h % 2], b * (8 * NH) + 16 * (h // 2 + 1))
                pool.tensor_tensor(o_cat[rows, h // 2, :], o_cat[rows, h // 2, :], side[rows, :], ALU.mult
                                   ).then_inc(s_o_norm, 1)
                pool.wait_ge(s_o_norm, b * NH + (h + 1))

            def step_sum(b, s):
                h, kt = s // TT, s % TT
                total = key_sum[:, h % 2, :]
                pool.wait_ge(s_exp, b * STEPS + (s + 1))
                if kt == 1:
                    if h >= 2:
                        pool.wait_ge(s_recip_row, b * (16 * NH) + 16 * (h - 1))
                    pool.tensor_tensor(total, prob[:, 0, :], prob[:, 1, :], ALU.add).then_inc(s_sum, 1)
                else:
                    pool.wait_ge(s_sum, b * (NH * NSUM) + NSUM * h + (kt - 1))
                    pool.tensor_tensor(total, total, prob[:, s % 2, :], ALU.add).then_inc(s_sum, 1)

            def run(body):
                for s, (ahead, behind) in enumerate(zip(body.jobs.ahead, body.jobs.behind)):
                    if s < STEPS and s % TT:
                        step_sum(body.b, s)
                    if divided_at(s) is not None:
                        divide(body.b, s, divided_at(s))
                    for job in ahead + behind:
                        do(body, s, job)

            pool.memset(ident[:, :], 0.0).then_inc(s_build, 1)
            pool.memset(group[:, :], 1.0 / GC).then_inc(s_build, 1)
            pool.memset(power[:, :], -0.5).then_inc(s_build, 1)
            pool.wait_ge(s_build, 3)
            pool.affine_select(out=ident[:, :], in_=ident[:, :], compare_op=ALU.not_equal, fill=1.0, base=0,
                               pattern=[[-1, P]], channel_multiplier=1).then_inc(s_const, 1)
            blocks = group[:, :].rearrange("p (g c) -> p g c", c=GC)
            pool.affine_select(out=blocks, in_=blocks, compare_op=ALU.is_ge, fill=0.0, base=0,
                               pattern=[[-GC, P // GC], [0, GC]], channel_multiplier=1).then_inc(s_build, 1)
            pool.wait_ge(s_build, 4)
            pool.affine_select(out=blocks, in_=blocks, compare_op=ALU.is_ge, fill=0.0, base=GC - 1,
                               pattern=[[GC, P // GC], [0, GC]], channel_multiplier=-1).then_inc(s_const, 1)
            pool.wait_ge(s_bias, 6)
            for job in FIRST.ahead[0]:
                do(first, 0, job)
            with pool.Fori(0, BATCH - 1) as b:
                run(looped(b))
            run(last)


_INS = {"x": "x", "L0_conv_gamma": "gamma", "L0_conv_beta": "beta", "L0_conv_w_qkv": "w_qkv",
        "L0_conv_b_qkv": "b_qkv", "L0_conv_w_out": "w_out", "L0_conv_b_out": "b_out"}


def kernel(**inputs):
    import numpy as np
    import concourse.bacc as bacc
    from concourse.bass_utils import run_bass_kernel_spmd

    nc = bacc.Bacc("TRN2", target_bir_lowering=False, num_devices=1)
    arrays, args = {}, {}
    for name, arg in _INS.items():
        a = np.ascontiguousarray(inputs[name])
        arrays[f"in_{arg}"] = a
        args[arg] = nc.dram_tensor(f"in_{arg}", a.shape, mybir.dt.from_np(a.dtype), kind="ExternalInput").ap()
    out = nc.dram_tensor("out_0", (BATCH, HH, WW, C), F32, kind="ExternalOutput").ap()
    build(nc, out=out, **args)
    r = run_bass_kernel_spmd(nc, [arrays], core_ids=[0])
    return r.results[0]["out_0"]
```

```python
from contextlib import ExitStack

import concourse.bass as bass
from concourse import mybir

F32 = mybir.dt.float32
F32R = mybir.dt.float32r
ALU = mybir.AluOpType
ACT = mybir.ActivationFunctionType
AX_X = mybir.AxisListType.X

P = 128
BATCH, HH, WW, C = 16, 32, 32, 512
L = HH * WW
D = 64
NH = C // D
NPAIR = NH // 2
CT = C // P
TT = L // P
HALF = 512
NHALF = L // HALF
GROUPS = 32
GC = C // GROUPS
EPS = 1e-5
SCALE = 1.0 / 8.0
STEPS = NH * TT
LAG = 2
NSLOT = 4
NRES = 4
QK_ORDER = [(1, 0), (1, 1), (0, 0), (0, 1)]
QK_ITEMS = len(QK_ORDER)
EARLY = [(1, *QK_ORDER[0])]
BIG = ("qk", "v", "out")
NO_BANK = ("statistics", "scale", "normalize")
STEP_COST, PART_COST = 1.1, 0.9
COST = {"x": 0.5, "group_mean": 0.1, "group_var": 0.1, "max": 0.2, "max_row": 0.2, "denominator": 1.8,
        "reciprocal_row": 0.2, "qk": PART_COST, "v": PART_COST, "out": PART_COST}
READ = {"x": 0.96, "group_mean": 0.42, "group_var": 0.3, "qk": 2.86, "v": 1.27, "max": 0.96, "max_row": 0.28,
        "denominator": 0.12, "reciprocal_row": 1.12, "out": 0.4}


def of_next(job):
    kind, n = job[0], job[1]
    return kind == "qk" and (n == 0 or job[1:4] in EARLY) or kind in ("max", "max_row") and n < 2


def whole(job, *inside):
    entries = []
    for ct in range(CT - 1):
        entries.append(("part", job, ct))
        entries += inside[ct] if ct < len(inside) else []
    return entries + [job]


def schedule(prepare_next):
    ahead = [[] for _ in range(STEPS + 1)]
    behind = [[] for _ in range(STEPS + 1)]
    second = set()

    def project(jobs, start):
        for i, job in enumerate(jobs):
            entries = whole(job)
            behind[start + 2 * i] += entries[:2]
            behind[start + 2 * i + 1] += entries[2:]
            second.add(start + 2 * i + 1)

    def maxima(h, steps):
        for qt, s in enumerate(steps):
            job0, job1 = ("max", h, qt, 0), ("max", h, qt, 1)
            if s in second:
                behind[s] = [job0, *behind[s][:1], job1, *behind[s][1:]]
                continue
            ahead[s].append(job0)
            behind[s].insert(len(behind[s]) if s + 1 in second else 0, job1)

    def qk_jobs(pair):
        return [("qk", pair, *item) for item in QK_ORDER]

    for pair in range(1, NPAIR):
        project([job for job in qk_jobs(pair) if job[1:] not in EARLY], 0 if pair == 1 else 16 * pair - 18)
    if prepare_next:
        project(qk_jobs(0), 52)
        maxima(0, range(59, STEPS))
    for h in range(2, NH):
        at = 8 * (h - 1) - 2
        maxima(h, range(at, at + 8))
        behind[at + 8].append(("max_row", h))
    if prepare_next:
        for tt in range(TT):
            behind[37 + tt].append(("x", tt))
        for i in range(CT):
            behind[37 + TT // 2 + i].append(("statistics", i, 0))
        for i in range(CT):
            behind[37 + TT + i // 2].append(("statistics", i, 1))
        behind[47].append(("group_mean",))
        behind[48].append(("group_var",))
        behind[49].append(("scale",))
        for i in range(CT):
            behind[50 + i // 2].append(("normalize", i))
    for h in range(NH - 1):
        at = 8 * h + 10
        behind[at] = ahead[at] + behind[at]
        ahead[at] = [("denominator", h)]
        behind[at + 1].append(("reciprocal_row", h))
    tail = ahead[STEPS]
    if prepare_next:
        def with_maxima(job, h, qt, before=()):
            half0, half1 = [[("max", h, qt, i)] for i in range(NHALF)]
            if job[0] == "out" and job[1] > 0:
                return whole(job, half0, [], half1)
            return whole(job, list(before), half0, half1)
        tail += whole(("v", 0)) + with_maxima(("v", 1), 0, 5) + [("denominator", NH - 1)]
        tail += with_maxima(("v", 2), 0, 6) + with_maxima(("v", 3), 0, 7, [("reciprocal_row", NH - 1)])
        tail += whole(("qk", *EARLY[0]), [], [("max_row", 0)]) + whole(("v", 4))
        for tt in range(TT):
            tail += with_maxima(("out", tt), 1, tt)
        tail += whole(("v", 5), [("max_row", 1)]) + whole(("v", 6)) + whole(("v", 7))
    else:
        tail += [("denominator", NH - 1), ("reciprocal_row", NH - 1)]
        for tt in range(TT):
            tail += whole(("out", tt))
    return ahead, behind


def first_schedule():
    jobs = [("x", tt) for tt in range(TT)] + [("statistics", ct, i) for i in range(NHALF) for ct in range(CT)]
    jobs += [("group_mean",), ("group_var",), ("scale",)] + [("normalize", ct) for ct in range(CT)]
    for item in QK_ORDER:
        jobs += whole(("qk", 0, *item))
    for h in range(2):
        for tt in range(TT):
            maxima = [[("max", h, tt, i)] for i in range(NHALF)]
            jobs += whole(("v", tt), maxima[0], [], maxima[1]) if h == 0 else maxima[0] + maxima[1]
        jobs += [("max_row", h)]
        if h == 0:
            for item in EARLY:
                jobs += whole(("qk", *item))
    return [jobs], [[]]


class Jobs:

    def __init__(self, schedule):
        self.ahead, self.behind = schedule
        self.bank, self.no, self.total = {}, {}, [0, 0]
        now, free, held = 0.0, [0.0, 0.0], None
        for a, b in zip(self.ahead, self.behind):
            now += STEP_COST
            for n, entry in enumerate(a + b):
                if n == len(a):
                    now += STEP_COST
                if entry[0] in NO_BANK:
                    continue
                part = entry[0] == "part"
                job = entry[1] if part else entry
                if job not in self.bank:
                    bank = 1 - held if held is not None else 0 if free[0] <= free[1] else 1
                    self.bank[job], self.no[job] = bank, self.total[bank]
                    self.total[bank] += 1
                bank = self.bank[job]
                now = max(now, free[bank]) + (PART_COST if part else COST[job[0]])
                if job[0] in BIG:
                    held = bank if part else None
                if not part:
                    free[bank] = now + READ[job[0]]


FIRST = Jobs(first_schedule())
LOOP = Jobs(schedule(True))
LAST = Jobs(schedule(False))


class Body:

    def __init__(self, b, prepares, jobs, loops):
        self.b = b
        self.prepares = prepares
        self.jobs, self.loops = jobs, loops

    def bank(self, job):
        return self.jobs.bank[job[1] if job[0] == "part" else job]

    def before(self, bank):
        return 0 if self.loops is None else self.loops * LOOP.total[bank] + FIRST.total[bank]

    def free(self, job):
        return self.before(self.bank(job)) + self.jobs.no[job]

    def done(self, job):
        return self.before(self.bank(job)) + (self.jobs.no[job] + 1)


def build(nc, x, gamma, beta, w_qkv, b_qkv, w_out, b_out, out):
    x_flat = x.rearrange("b h w c -> (b h w c)")
    out_flat = out.rearrange("b h w c -> (b h w c)")

    with ExitStack() as ctx:
        def sb(name, shape, dt=F32):
            return ctx.enter_context(nc.sbuf_tensor(name, shape, dt))

        def ps(name, shape):
            return ctx.enter_context(nc.psum_tensor(name, shape, F32))

        def sem(name):
            return ctx.enter_context(nc.semaphore(name))

        wqkv = sb("wqkv", [P, CT, 3 * C])
        wout = sb("wout", [P, CT, C])
        ident = sb("ident", [P, P])
        group = sb("group", [P, P])
        ones = sb("ones", [P, 2])
        bias_all = sb("bias_all", [P, C])
        bv = sb("bv", [P, CT])
        gamma_c = sb("gamma_c", [P, CT])
        beta_c = sb("beta_c", [P, CT])
        bqk = sb("bqk", [P, 2, NPAIR])
        bqk_odd = sb("bqk_odd", [D, 2, NPAIR])
        xt = sb("xt", [P, 2, C])
        xn = sb("xn", [P, CT, L])
        bn = sb("bn", [P, CT, NHALF, 6])
        carrier = sb("carrier", [P, 1])
        chan = sb("chan", [P, CT, 2])
        grp = sb("grp", [P, CT, 2])
        dev = sb("dev", [P, CT])
        dev2 = sb("dev2", [P, CT])
        gvar = sb("gvar", [P, CT])
        power = sb("power", [P, CT])
        rstd = sb("rstd", [P, CT])
        mul = sb("mul", [P, CT])
        off = sb("off", [P, CT])
        moff = sb("moff", [P, CT])
        k_stack = sb("k_stack", [P, NSLOT, L], F32R)
        k_aug = sb("k_aug", [D + 1, NSLOT, L], F32R)
        q_twin = sb("q_twin", [P, NSLOT, L], F32R)
        q_aug = sb("q_aug", [D + 1, NSLOT, L], F32R)
        v_stack = sb("v_stack", [P, TT, NPAIR, 4, D], F32R)
        mx = sb("mx", [P, TT, NHALF])
        mrow = sb("mrow", [P, TT])
        neg_max = sb("neg_max", [TT, P], F32R)
        prob = sb("prob", [P, 2, L])
        prob_hi = sb("prob_hi", [P, 2, L], F32R)
        prob_lo = sb("prob_lo", [P, 2, L], F32R)
        key_sum = sb("key_sum", [P, 2, L])
        recip = sb("recip", [P, TT])
        recip_t = sb("recip_t", [TT, P])
        side = sb("side", [P, L])
        o_cat = sb("o_cat", [P, NPAIR, L])

        recip_dram = nc.dram_tensor("recip_dram", [2, TT, P], F32, kind="Internal").ap()

        def res(tt):
            return prob[:, (tt % NRES) // 2, (tt % 2) * HALF:(tt % 2 + 1) * HALF]

        scores = ps("scores", [P, 2, L])
        pv = ps("pv", [P, L])
        spare = ps("spare", [P, 2, HALF])

        s_build = sem("s_build")
        s_load = sem("s_load")
        s_const = sem("s_const")
        s_x_load = [sem(f"s_x_load{i}") for i in range(2)]
        s_stat = sem("s_stat")
        s_rstd = sem("s_rstd")
        s_xn = [sem(f"s_xn{i}") for i in range(2)]
        s_filled = [sem(f"s_filled{i}") for i in range(2)]
        s_taken = [sem(f"s_taken{i}") for i in range(2)]
        s_qk_hi = sem("s_qk_hi")
        s_second_hi = [sem(f"s_second_hi{i}") for i in range(2)]
        s_v_hi = sem("s_v_hi")
        s_bias = sem("s_bias")
        s_bias_ps = sem("s_bias_ps")
        s_rowmax = sem("s_rowmax")
        s_shift = sem("s_shift")
        s_scores = sem("s_scores")
        s_exp = sem("s_exp")
        s_hi = sem("s_hi")
        s_lo = sem("s_lo")
        s_sum = sem("s_sum")
        s_pv = sem("s_pv")
        s_o_low = sem("s_o_low")
        s_o = sem("s_o")
        s_recip_row = sem("s_recip_row")
        s_recip_all = [sem(f"s_recip_all{i}") for i in range(2)]
        s_o_norm = sem("s_o_norm")
        s_res = [sem(f"s_res{i}") for i in range(NRES)]
        s_res_bias = sem("s_res_bias")
        s_store = [sem(f"s_store{i}") for i in range(NRES)]

        NLOAD = 16 * (2 * CT + 2 + 2 * 2 + 2)
        NCONST = 2 + 2
        NSTAT = 7
        NSUM = TT - 1

        first = Body(None, 0, FIRST, None)
        last = Body(BATCH - 1, None, LAST, BATCH - 1)

        def looped(b):
            return Body(b, b + 1, LOOP, b)

        def half(i):
            return slice(i * HALF, (i + 1) * HALF)

        def tile(i):
            return slice(i * P, (i + 1) * P)

        def tokens(dram, start):
            return dram[bass.ds(start, P * C)].rearrange("(p c) -> p c", c=C)

        def image_of(body, job):
            return body.prepares if of_next(job) else body.b

        def last_of_banks(body, jobs):
            return [[job for job in jobs if body.bank(job) == i][-1] for i in range(2)
                    if any(body.bank(job) == i for job in jobs)]

        def qk_hi_value(body, job):
            _, pair, which, i = job
            return image_of(body, job) * (NPAIR * QK_ITEMS) + (QK_ITEMS * pair + QK_ORDER.index((which, i)) + 1)

        def divided_at(s):
            return s // TT - 2 if s % TT == 0 and s >= 2 * TT else None

        block = ctx.enter_context(nc.Block())

        @block.sync
        def _(sp):
            def early(value):
                return value if isinstance(value, int) else sp.snap(value)

            def start_of(n, tt):
                return early(n * (L * C) + tt * P * C)

            def load_x(body, tt):
                n = body.prepares
                start = start_of(n, tt)
                if tt >= 2:
                    job = ("x", tt - 2)
                    sp.wait_ge(s_taken[body.bank(job)], body.done(job))
                elif body is not first:
                    sp.wait_ge(s_v_hi, n * TT)
                sp.dma_start(xt[:, tt % 2, :], tokens(x_flat, start)).then_inc(s_x_load[tt % 2], 16)

            def second_hi(body, job):
                _, pair, which, i = job
                slots = slice(2 * pair % NSLOT, 2 * pair % NSLOT + 2)
                sp.wait_ge(s_qk_hi, qk_hi_value(body, job))
                sp.dma_start((q_twin[D:P, slots, half(i)], k_aug[0:D, slots, half(i)])[which].bitcast(F32),
                             (q_twin, k_stack)[which][0:D, slots, half(i)].bitcast(F32)
                             ).then_inc(s_second_hi[(which, i) == QK_ORDER[-1]], 16)

            def shift_row(body, job):
                h = job[1]
                sp.wait_ge(s_taken[body.bank(job)], body.done(job))
                sp.dma_start(q_aug[D:D + 1, h % NSLOT, :].bitcast(F32).rearrange("a (t p) -> a t p", p=P),
                             neg_max[:, :].bitcast(F32)
                             ).then_inc(s_shift, 16)

            def recip_rows(body, job):
                h = job[1]
                rows = slice(D * (h % 2), D * (h % 2) + D)
                sp.wait_ge(s_taken[body.bank(job)], body.done(job))
                sp.dma_start(recip_dram[h % 2, :, :], recip_t[:, :]).then_inc(s_recip_row, 16)
                sp.wait_ge(s_recip_row, body.b * (16 * NH) + 16 * (h + 1))
                sp.dma_start(side[rows, :],
                             recip_dram[h % 2, :, :].rearrange("(a t) p -> a (t p)", a=1).broadcast_to([D, L])
                             ).then_inc(s_recip_all[h % 2], 16)

            def load_res(body, tt):
                b = body.b
                start = start_of(b, tt)
                if tt < NRES:
                    steps = early(b * STEPS + STEPS)
                    sums = early(b * (NH * NSUM) + NH * NSUM)
                    sp.wait_ge(s_hi, steps)
                    sp.wait_ge(s_lo, steps)
                    sp.wait_ge(s_sum, sums)
                else:
                    sp.wait_ge(s_store[tt % NRES], b * 32 + 16)
                sp.dma_start(res(tt), tokens(x_flat, start)).then_inc(s_res[tt % NRES], 16)

            def store(body, job):
                tt = job[1]
                start = start_of(body.b, tt)
                sp.wait_ge(s_taken[body.bank(job)], body.done(job))
                sp.dma_start(tokens(out_flat, start), res(tt)).then_inc(s_store[tt % NRES], 16)

            def run(body):
                if body is not last:
                    load_x(body, 0)
                    load_x(body, 1)
                for s, (ahead, behind) in enumerate(zip(body.jobs.ahead, body.jobs.behind)):
                    if s == STEPS:
                        for tt in range(NRES):
                            load_res(body, tt)
                    for job in ahead + behind:
                        if job[0] == "x" and job[1] + 2 < TT:
                            load_x(body, job[1] + 2)
                        if job[0] == "qk":
                            second_hi(body, job)
                        if job[0] == "max_row":
                            shift_row(body, job)
                        if job[0] == "reciprocal_row":
                            recip_rows(body, job)
                        if job[0] == "out":
                            store(body, job)
                            if job[1] + NRES < TT:
                                load_res(body, job[1] + NRES)

            for ct in range(CT):
                sp.dma_start(wqkv[:, ct, :], w_qkv[tile(ct), :]).then_inc(s_load, 16)
                sp.dma_start(wout[:, ct, :], w_out[tile(ct), :]).then_inc(s_load, 16)
            with nc.allow_non_contiguous_dma("a few small vectors, once"):
                sp.dma_start(gamma_c[:, :], gamma.rearrange("(t p) -> p t", p=P)).then_inc(s_load, 16)
                sp.dma_start(beta_c[:, :], beta.rearrange("(t p) -> p t", p=P)).then_inc(s_load, 16)
                sp.dma_start(bv[:, :], b_qkv[2 * C:3 * C].rearrange("(t p) -> p t", p=P)).then_inc(s_load, 16)
                for j in range(2):
                    part = b_qkv[j * C:(j + 1) * C].rearrange("(t p) -> p t", p=P)
                    sp.dma_start(bqk[:, j, :], part).then_inc(s_load, 16)
                    sp.dma_start(bqk_odd[:, j, :], part[D:P, :]).then_inc(s_load, 16)
            sp.dma_start(bias_all[:, :], b_out.rearrange("(a c) -> a c", a=1).broadcast_to([P, C])
                         ).then_inc(s_load, 16)
            run(first)
            with sp.Fori(0, BATCH - 1) as b:
                run(looped(b))
            run(last)
            for i in range(NRES):
                sp.wait_ge(s_store[i], BATCH * 32)

        @block.tensor
        def _(pe):
            def big(body, job, ct):
                kind, n = job[0], job[1]
                bank = spare[:, body.bank(job), :]
                if kind == "qk":
                    _, pair, which, i = job
                    stationary = wqkv[:, ct, which * C + pair * P:which * C + (pair + 1) * P]
                    moving = xn[:, ct, half(i)]
                elif kind == "v":
                    stationary, moving = xn[:, ct, tile(n)], wqkv[:, ct, 2 * C:3 * C]
                else:
                    stationary, moving = o_cat[:, ct, tile(n)], wout[:, ct, :]
                mm = pe.matmul(bank, stationary, moving, start=(ct == 0), stop=(ct == CT - 1), skip_group_check=True)
                if ct == CT - 1:
                    mm.then_inc(s_filled[body.bank(job)], 1)

            def wait_free(body, job):
                if not (body is first and body.jobs.no[job] == 0):
                    pe.wait_ge(s_taken[body.bank(job)], body.free(job))

            def do(body, job):
                kind = job[0]
                if kind in NO_BANK:
                    return
                if kind in BIG:
                    big(body, job, CT - 1)
                    return
                if kind == "part":
                    _, job, ct = job
                    if ct == 0:
                        wait_free(body, job)
                        if job[:2] == ("qk", 0):
                            for i in range(2):
                                pe.wait_ge(s_xn[i], body.prepares * (CT // 2) + CT // 2)
                        if job == ("out", 0):
                            pe.wait_ge(s_o_norm, body.b * NH + NH)
                    big(body, job, ct)
                    return
                bank = spare[:, body.bank(job), :]
                wait_free(body, job)
                if kind == "x":
                    tt = job[1]
                    pe.wait_ge(s_x_load[tt % 2], body.prepares * (8 * TT) + 16 * (tt // 2 + 1))
                    for ct in range(CT):
                        mm = pe.transpose(bank[:, tile(ct)], xt[:, tt % 2, tile(ct)], ident[:, :])
                elif kind == "group_mean":
                    pe.wait_ge(s_stat, body.prepares * NSTAT + 2)
                    mm = pe.matmul(bank[:, 0:2 * CT], group[:, :], chan[:, :, :].rearrange("p t s -> p (t s)"),
                                   start=True, stop=True)
                elif kind == "group_var":
                    pe.wait_ge(s_stat, body.prepares * NSTAT + 4)
                    mm = pe.matmul(bank[:, 0:CT], group[:, :], dev2[:, :], start=True, stop=True)
                elif kind == "max":
                    _, h, qt, i = job
                    if h % 2 == 0 and qt % (TT // 2) == 0 and i == 0:
                        late = qt > 0
                        made = [("qk", h // 2, *item) for item in QK_ORDER if (h // 2, *item) not in EARLY]
                        made = made[-1:] if late else made[:-1]
                        other = [j for j in made if body.bank(j) != body.bank(job)]
                        if other:
                            pe.wait_ge(s_taken[body.bank(other[-1])], body.done(other[-1]))
                        count = 16 if late else 16 * (QK_ITEMS - 1)
                        pe.wait_ge(s_second_hi[late], (image_of(body, job) * NPAIR + (h // 2 + 1)) * count)
                    mm = pe.matmul(bank, q_twin[:, h % NSLOT, tile(qt)], k_stack[:, h % NSLOT, half(i)],
                                   start=True, stop=True)
                elif kind == "max_row":
                    h = job[1]
                    pe.wait_ge(s_rowmax, image_of(body, job) * NH + (h + 1))
                    mm = pe.transpose(bank[0:TT, 0:P], mrow[:, :], ident[:, :])
                elif kind == "denominator":
                    h = job[1]
                    pe.wait_ge(s_sum, body.b * (NH * NSUM) + NSUM * (h + 1))
                    for qt in range(TT):
                        mm = pe.matmul(bank[:, qt:qt + 1], key_sum[:, h % 2, tile(qt)], ones[:, 0:1],
                                       start=True, stop=True)
                elif kind == "reciprocal_row":
                    pe.wait_ge(s_o, body.b * NH + (job[1] + 1))
                    made = ("denominator", job[1])
                    if body.bank(made) != body.bank(job):
                        pe.wait_ge(s_taken[body.bank(made)], body.done(made))
                    mm = pe.transpose(bank[0:TT, 0:P], recip[:, :], ident[:, :])
                mm.then_inc(s_filled[body.bank(job)], 1)

            def step_scores(b, s):
                h, kt = s // TT, s % TT
                slot = h % NSLOT
                if kt == 0:
                    pe.wait_ge(s_shift, b * (16 * NH) + 16 * (h + 1))
                if s >= 2:
                    pe.wait_ge(s_exp, b * STEPS + (s - 1))
                for i in range(NHALF):
                    pe.matmul(scores[:, s % 2, half(i)], k_stack[:, slot, tile(kt)], q_twin[:, slot, half(i)],
                              start=True, stop=False)
                for i in range(NHALF):
                    mm = pe.matmul(scores[:, s % 2, half(i)], k_aug[:, slot, tile(kt)], q_aug[:, slot, half(i)],
                                   start=False, stop=True)
                mm.then_inc(s_scores, 1)

            def step_pv(b, s):
                h, kt = s // TT, s % TT
                if kt == 0 and h > 0:
                    pe.wait_ge(s_o, b * NH + h)
                v = v_stack[:, kt, h // 2, 2 * (h % 2):2 * (h % 2) + 2, :].rearrange("p a d -> p (a d)")
                pe.wait_ge(s_hi, b * STEPS + (s + 1))
                for i in range(NHALF):
                    pe.matmul(pv[:, half(i)], v, prob_hi[:, s % 2, half(i)], start=(kt == 0), stop=False)
                pe.wait_ge(s_lo, b * STEPS + (s + 1))
                for i in range(NHALF):
                    mm = pe.matmul(pv[:, half(i)], v, prob_lo[:, s % 2, half(i)], start=False,
                                   stop=(kt == TT - 1))
                mm.then_inc(s_pv, 1)

            def run(body):
                last_pv = (0, 1) if body is last else (0, 2)
                for s, (ahead, behind) in enumerate(zip(body.jobs.ahead, body.jobs.behind)):
                    if s < STEPS:
                        step_scores(body.b, s)
                    if s == 0:
                        for bank in range(2):
                            pe.wait_ge(s_taken[bank], body.before(bank))
                    if s == STEPS:
                        pe.wait_ge(s_exp, body.b * STEPS + STEPS)
                    for n, job in enumerate(ahead):
                        if s == STEPS and n in last_pv:
                            step_pv(body.b, s - LAG + last_pv.index(n))
                        do(body, job)
                    if LAG <= s < STEPS:
                        step_pv(body.b, s - LAG)
                    for job in behind:
                        do(body, job)

            pe.wait_ge(s_load, NLOAD)
            pe.wait_ge(s_const, NCONST)
            pe.wait_ge(s_bias, 5)
            for ct in range(CT):
                mm = pe.matmul(pv[:, half(0)], side[:, tile(ct)], wout[:, ct, :],
                               start=(ct == 0), stop=(ct == CT - 1))
            mm.then_inc(s_bias_ps, 1)
            for job in FIRST.ahead[0]:
                do(first, job)
            with pe.Fori(0, BATCH - 1) as b:
                run(looped(b))
            run(last)

        @block.scalar
        def _(act):
            def do(body, job):
                kind = job[0]
                if kind == "normalize" and job[1] % 2 == 1:
                    ct = job[1]
                    if ct == 1:
                        act.wait_ge(s_stat, body.prepares * NSTAT + 7)
                    act.activation(xn[:, ct, :], xn[:, ct, :], ACT.Identity, bias=off[:, ct:ct + 1],
                                   scale=mul[:, ct:ct + 1]).then_inc(s_xn[1], 1)
                if kind in NO_BANK or kind == "part":
                    return
                bank = spare[:, body.bank(job), :]
                taken = s_taken[body.bank(job)]
                if kind in ("x", "qk", "v", "max_row", "reciprocal_row"):
                    act.wait_ge(s_filled[body.bank(job)], body.done(job))
                if kind == "x":
                    act.activation(xn[:, :, tile(job[1])], bank.rearrange("p (t c) -> p t c", t=CT), ACT.Copy
                                   ).then_inc(taken, 1)
                if kind == "qk":
                    _, pair, which, i = job
                    for e in range(2):
                        rows = slice(D * e, D * e + D)
                        hi = act.activation((q_twin, k_stack)[which][0:D, (2 * pair + e) % NSLOT, half(i)],
                                            bank[rows, :], ACT.Identity, bias=bqk[rows, which, pair:pair + 1])
                    hi.then_inc(s_qk_hi, 1)
                if kind == "v":
                    act.activation(v_stack[:, job[1], :, 0::3, :],
                                   bank.rearrange("p (a e d) -> p a e d", e=2, d=D), ACT.Copy).then_inc(s_v_hi, 1)
                if kind == "max_row":
                    h = job[1]
                    if not (body is first and h == 0):
                        act.wait_ge(s_shift, image_of(body, job) * (16 * NH) + 16 * h)
                    act.activation(neg_max[:, :], bank[0:TT, 0:P], ACT.Copy, scale=-1.0).then_inc(taken, 1)
                if kind == "reciprocal_row":
                    if job[1] > 0:
                        act.wait_ge(s_recip_row, body.b * (16 * NH) + 16 * job[1])
                    act.activation(recip_t[:, :], bank[0:TT, 0:P], ACT.Copy).then_inc(taken, 1)

            def step_exp(b, s):
                act.wait_ge(s_scores, b * STEPS + (s + 1))
                if s >= 2:
                    h, kt = (s - 2) // TT, (s - 2) % TT
                    act.wait_ge(s_lo, b * STEPS + (s - 1))
                    act.wait_ge(s_sum, b * (NH * NSUM) + NSUM * h + max(kt, 1))
                act.activation(prob[:, s % 2, :], scores[:, s % 2, :], ACT.Exp, scale=SCALE).then_inc(s_exp, 1)

            def step_hi(b, s):
                act.wait_ge(s_exp, b * STEPS + (s + 1))
                if s >= 2:
                    act.wait_ge(s_pv, b * STEPS + (s - 1))
                act.activation(prob_hi[:, s % 2, :], prob[:, s % 2, :], ACT.Copy).then_inc(s_hi, 1)

            def take_o_low(b, h):
                act.wait_ge(s_pv, b * STEPS + TT * (h + 1))
                if h >= 2:
                    act.wait_ge(s_o_norm, b * NH + (h - 1))
                to, frm = D * (h % 2), D * (1 - h % 2)
                act.activation(side[to:to + D, :], pv[frm:frm + D, :], ACT.Copy).then_inc(s_o_low, 1)

            def run(body):
                for s, (ahead, behind) in enumerate(zip(body.jobs.ahead, body.jobs.behind)):
                    if s < STEPS:
                        step_exp(body.b, s)
                        if s > TT and (s - LAG + 1) % TT == 0:
                            take_o_low(body.b, (s - LAG + 1) // TT - 1)
                        step_hi(body.b, s)
                    else:
                        take_o_low(body.b, NH - 1)
                    for job in ahead + behind:
                        do(body, job)
                if body is not last:
                    for i in range(NRES):
                        act.wait_ge(s_store[i], body.b * 32 + 32)

            act.wait_ge(s_load, NLOAD)
            for job in FIRST.ahead[0]:
                do(first, job)
            with act.Fori(0, BATCH - 1) as b:
                run(looped(b))
            run(last)

        @block.vector
        def _(dve):
            def do(body, job):
                kind, n = job[0], body.prepares
                if kind == "part":
                    return
                if kind not in NO_BANK:
                    bank = spare[:, body.bank(job), :]
                    taken = s_taken[body.bank(job)]
                if kind in ("group_mean", "group_var", "max", "denominator", "out"):
                    dve.wait_ge(s_filled[body.bank(job)], body.done(job))
                if kind == "statistics":
                    _, ct, i = job
                    if ct == 0:
                        tiles = [("x", tt) for tt in range(i * TT // 2, (i + 1) * TT // 2)]
                        for x_job in last_of_banks(body, tiles):
                            dve.wait_ge(s_taken[body.bank(x_job)], body.done(x_job))
                    a = dve.bn_stats(bn[:, ct, i, :], xn[:, ct, half(i)])
                    if ct == CT - 1 and i == NHALF - 1:
                        a.then_inc(s_stat, 1)
                        dve.wait_ge(s_stat, n * NSTAT + 1)
                        dve.memset(carrier[:, :], 0.0)
                        for j in range(CT):
                            a = dve.bn_aggr(chan[:, j, :], bn[:, j, :, :])
                        a.then_inc(s_stat, 1)
                if kind == "group_mean":
                    dve.tensor_copy(grp[:, :, :].rearrange("p t s -> p (t s)"), bank[:, 0:2 * CT]).then_inc(taken, 1)
                    dve.wait_ge(taken, body.done(job))
                    dve.tensor_tensor(dev[:, :], chan[:, :, 0], grp[:, :, 0], ALU.subtract).then_inc(s_stat, 1)
                    dve.wait_ge(s_stat, n * NSTAT + 3)
                    dve.tensor_tensor(dev2[:, :], dev[:, :], dev[:, :], ALU.mult).then_inc(s_stat, 1)
                if kind == "group_var":
                    dve.scalar_tensor_tensor(out=gvar[:, :], in0=bank[:, 0:CT], scalar=EPS, in1=grp[:, :, 1],
                                             op0=ALU.add, op1=ALU.add).then_inc(taken, 1)
                if kind == "scale":
                    dve.wait_ge(s_rstd, n + 1)
                    dve.tensor_tensor(mul[:, :], rstd[:, :], gamma_c[:, :], ALU.mult).then_inc(s_stat, 1)
                    dve.wait_ge(s_stat, n * NSTAT + 5)
                    dve.tensor_tensor(moff[:, :], grp[:, :, 0], mul[:, :], ALU.mult).then_inc(s_stat, 1)
                    dve.wait_ge(s_stat, n * NSTAT + 6)
                    dve.tensor_tensor(off[:, :], beta_c[:, :], moff[:, :], ALU.subtract).then_inc(s_stat, 1)
                if kind == "normalize" and job[1] % 2 == 0:
                    ct = job[1]
                    if ct == 0:
                        dve.wait_ge(s_stat, n * NSTAT + 7)
                    dve.tensor_scalar(xn[:, ct, :], xn[:, ct, :], mul[:, ct:ct + 1], off[:, ct:ct + 1],
                                      ALU.mult, ALU.add).then_inc(s_xn[0], 1)
                if kind == "qk":
                    _, pair, which, i = job
                    dve.wait_ge(s_qk_hi, qk_hi_value(body, job))
                    for e in range(2):
                        slot = (2 * pair + e) % NSLOT
                        hi = (q_twin, k_stack)[which][0:D, slot, half(i)]
                        lo = (q_aug[0:D, slot, half(i)], k_stack[D:P, slot, half(i)])[which]
                        a = dve.scalar_tensor_tensor(out=lo, in0=bank[D * e:D * e + D, :],
                                                     scalar=(bqk, bqk_odd)[e][0:D, which, pair:pair + 1], in1=hi,
                                                     op0=ALU.add, op1=ALU.subtract)
                    a.then_inc(taken, 1)
                if kind == "v":
                    tt = job[1]
                    dve.wait_ge(s_v_hi, n * TT + (tt + 1))
                    dve.tensor_tensor(v_stack[:, tt, :, 1:3, :], bank.rearrange("p (a e d) -> p a e d", e=2, d=D),
                                      v_stack[:, tt, :, 0::3, :], ALU.subtract).then_inc(taken, 1)
                if kind == "max":
                    _, h, qt, i = job
                    if qt == 0 and i == 0 and not (body is first and h == 0):
                        dve.wait_ge(s_rowmax, image_of(body, job) * NH + h)
                    dve.tensor_reduce(mx[:, qt, i:i + 1], bank, AX_X, ALU.max).then_inc(taken, 1)
                    if qt == TT - 1 and i == NHALF - 1:
                        for end in last_of_banks(body, [("max", h, j // NHALF, j % NHALF)
                                                        for j in range(TT * NHALF)]):
                            dve.wait_ge(s_taken[body.bank(end)], body.done(end))
                        dve.tensor_tensor(mrow[:, :], mx[:, :, 0], mx[:, :, 1], ALU.max).then_inc(s_rowmax, 1)
                if kind == "denominator":
                    dve.reciprocal(recip[:, :], bank[:, 0:TT]).then_inc(taken, 1)
                if kind == "out":
                    tt = job[1]
                    dve.wait_ge(s_res_bias, body.b * TT + (tt + 1))
                    dve.tensor_tensor(res(tt), bank, res(tt), ALU.add).then_inc(taken, 1)

            def step_lo(b, s):
                dve.wait_ge(s_hi, b * STEPS + (s + 1))
                if s >= 2:
                    dve.wait_ge(s_pv, b * STEPS + (s - 1))
                dve.tensor_tensor(prob_lo[:, s % 2, :], prob[:, s % 2, :], prob_hi[:, s % 2, :], ALU.subtract
                                  ).then_inc(s_lo, 1)

            def add_o(b, h):
                rows = slice(D * (h % 2), D * (h % 2) + D)
                dve.wait_ge(s_o_low, b * NH + (h + 1))
                dve.tensor_tensor(o_cat[rows, h // 2, :], pv[rows, :], side[rows, :], ALU.add).then_inc(s_o, 1)

            def run(body):
                late = []
                for s, (ahead, behind) in enumerate(zip(body.jobs.ahead, body.jobs.behind)):
                    if s == STEPS:
                        for job in late:
                            do(body, job)
                        add_o(body.b, NH - 1)
                        for job in ahead:
                            do(body, job)
                        break
                    early = ahead + behind[:[job[0] for job in behind + [("part",)]].index("part")]
                    early = [job for job in early if job[0] == "max"]
                    if ahead and ahead[0][0] == "denominator":
                        early = late + ahead + early
                    else:
                        early = early[:1] + late + early[1:]
                    early += [job for job in behind if job[0] in ("statistics", "group_mean", "group_var")]
                    for job in early:
                        do(body, job)
                    if s > TT and (s - LAG + 1) % TT == 0:
                        add_o(body.b, (s - LAG + 1) // TT - 1)
                    late = [job for job in behind if job[0] == "qk"]
                    if late or s > TT and (s - LAG + 1) % TT == 0:
                        more = [job for job in behind if job[0] == "max" and job not in early]
                        for job in more:
                            do(body, job)
                        early += more
                    step_lo(body.b, s)
                    for job in ahead + behind:
                        if job not in early + late:
                            do(body, job)

            dve.memset(ones[:, :], 1.0).then_inc(s_const, 1)
            dve.memset(k_aug[D:D + 1, :, :].bitcast(F32), 1.0).then_inc(s_const, 1)
            dve.memset(side[:, half(1)], 1.0).then_inc(s_bias, 1)
            dve.wait_ge(s_load, NLOAD)
            dve.wait_ge(s_bias, 1)
            for ct in range(CT):
                dve.tensor_scalar(side[:, tile(ct)], side[:, half(1)][:, tile(0)], bv[:, ct:ct + 1], None, ALU.mult
                                  ).then_inc(s_bias, 1)
            dve.wait_ge(s_bias_ps, 1)
            dve.tensor_tensor(bias_all[:, :], pv[:, half(0)], bias_all[:, :], ALU.add).then_inc(s_bias, 1)
            for job in FIRST.ahead[0]:
                do(first, job)
            with dve.Fori(0, BATCH - 1) as b:
                run(looped(b))
            run(last)

        @block.gpsimd
        def _(pool):
            def do(body, s, job):
                kind, b = job[0], body.b
                if kind == "group_var":
                    pool.wait_ge(s_taken[body.bank(job)], body.done(job))
                    pool.tensor_tensor(rstd[:, :], gvar[:, :], power[:, :], ALU.pow).then_inc(s_rstd, 1)
                if kind == "reciprocal_row" and job[1] == NH - 1:
                    divide(b, s, NH - 1)
                if kind == "out":
                    tt = job[1]
                    pool.wait_ge(s_res[tt % NRES], b * 32 + 16 * (tt // NRES + 1))
                    pool.tensor_tensor(res(tt), res(tt), bias_all[:, :], ALU.add).then_inc(s_res_bias, 1)

            def divide(b, s, h):
                rows = slice(D * (h % 2), D * (h % 2) + D)
                pool.wait_ge(s_sum, b * (NH * NSUM) + NSUM * (s // TT) + s % TT)
                pool.wait_ge(s_o, b * NH + (h + 1))
                pool.wait_ge(s_recip_all[h % 2], b * (8 * NH) + 16 * (h // 2 + 1))
                pool.tensor_tensor(o_cat[rows, h // 2, :], o_cat[rows, h // 2, :], side[rows, :], ALU.mult
                                   ).then_inc(s_o_norm, 1)
                pool.wait_ge(s_o_norm, b * NH + (h + 1))

            def step_sum(b, s):
                h, kt = s // TT, s % TT
                total = key_sum[:, h % 2, :]
                pool.wait_ge(s_exp, b * STEPS + (s + 1))
                if kt == 1:
                    if h >= 2:
                        pool.wait_ge(s_recip_row, b * (16 * NH) + 16 * (h - 1))
                    pool.tensor_tensor(total, prob[:, 0, :], prob[:, 1, :], ALU.add).then_inc(s_sum, 1)
                else:
                    pool.wait_ge(s_sum, b * (NH * NSUM) + NSUM * h + (kt - 1))
                    pool.tensor_tensor(total, total, prob[:, s % 2, :], ALU.add).then_inc(s_sum, 1)

            def run(body):
                for s, (ahead, behind) in enumerate(zip(body.jobs.ahead, body.jobs.behind)):
                    if s < STEPS and s % TT:
                        step_sum(body.b, s)
                    if divided_at(s) is not None:
                        divide(body.b, s, divided_at(s))
                    for job in ahead + behind:
                        do(body, s, job)

            pool.memset(ident[:, :], 0.0).then_inc(s_build, 1)
            pool.memset(group[:, :], 1.0 / GC).then_inc(s_build, 1)
            pool.memset(power[:, :], -0.5).then_inc(s_build, 1)
            pool.wait_ge(s_build, 3)
            pool.affine_select(out=ident[:, :], in_=ident[:, :], compare_op=ALU.not_equal, fill=1.0, base=0,
                               pattern=[[-1, P]], channel_multiplier=1).then_inc(s_const, 1)
            blocks = group[:, :].rearrange("p (g c) -> p g c", c=GC)
            pool.affine_select(out=blocks, in_=blocks, compare_op=ALU.is_ge, fill=0.0, base=0,
                               pattern=[[-GC, P // GC], [0, GC]], channel_multiplier=1).then_inc(s_build, 1)
            pool.wait_ge(s_build, 4)
            pool.affine_select(out=blocks, in_=blocks, compare_op=ALU.is_ge, fill=0.0, base=GC - 1,
                               pattern=[[GC, P // GC], [0, GC]], channel_multiplier=-1).then_inc(s_const, 1)
            pool.wait_ge(s_bias, 6)
            for job in FIRST.ahead[0]:
                do(first, 0, job)
            with pool.Fori(0, BATCH - 1) as b:
                run(looped(b))
            run(last)


_INS = {"x": "x", "L0_conv_gamma": "gamma", "L0_conv_beta": "beta", "L0_conv_w_qkv": "w_qkv",
        "L0_conv_b_qkv": "b_qkv", "L0_conv_w_out": "w_out", "L0_conv_b_out": "b_out"}


def kernel(**inputs):
    import numpy as np
    import concourse.bacc as bacc
    from concourse.bass_utils import run_bass_kernel_spmd

    nc = bacc.Bacc("TRN2", target_bir_lowering=False, num_devices=1)
    arrays, args = {}, {}
    for name, arg in _INS.items():
        a = np.ascontiguousarray(inputs[name])
        arrays[f"in_{arg}"] = a
        args[arg] = nc.dram_tensor(f"in_{arg}", a.shape, mybir.dt.from_np(a.dtype), kind="ExternalInput").ap()
    out = nc.dram_tensor("out_0", (BATCH, HH, WW, C), F32, kind="ExternalOutput").ap()
    build(nc, out=out, **args)
    r = run_bass_kernel_spmd(nc, [arrays], core_ids=[0])
    return r.results[0]["out_0"]
```
